# Optimizing a Trainium2 kernel written in Bass

```python
import numpy as np
import jax
import jax.numpy as jnp

def _softmax(x, axis=-1):
    return jax.nn.softmax(x, axis=axis)
def _gelu(x):
    return jax.nn.gelu(x, approximate=True)
def _silu(x):
    return jax.nn.silu(x)
def _sigmoid(x):
    return jax.nn.sigmoid(x)
def _layernorm(x, axis=-1, eps=1e-5):
    m = jnp.mean(x, axis=axis, keepdims=True)
    v = jnp.var(x, axis=axis, keepdims=True)
    return (x - m) / jnp.sqrt(v + eps)
def _scatter_add(tgt, idx, src, axis=0):
    return tgt.at[idx].add(src)
def _segment_sum(src, seg, n):
    return jax.ops.segment_sum(src, seg, n)

kernel_name = 'mk_adj_preln_d1_adj_768_9c093e'

def setup_inputs(seed: int = 0):
    np.random.seed(seed)
    _w = jnp.asarray
    def _rec_inputs():
        import jax
        import jax.numpy as jnp
        _gk = jax.random.key(seed)
        x = -0.0004039 + 1 * jax.random.normal(jax.random.fold_in(_gk, 1), (128, 64, 768), jnp.float32)
        _a = jax.random.bernoulli(jax.random.fold_in(_gk, 2), 0.0625, (128, 64, 64))
        _af = _a.astype(jnp.float32)
        adj = _af
        return x, adj
    x, adj = _rec_inputs()
    def _L0_gnn_setup():
        import jax, jax.numpy as jnp
        import numpy as np
        B, S, H, L = (32, 512, 768, 2)

        def _layer_norm(z, a, b, eps=0.001):
            mu = jnp.mean(z, axis=-1, keepdims=True)
            sigma = jnp.std(z, axis=-1, keepdims=True, ddof=1)
            return (z - mu) / (sigma + eps) * a + b
        key = jax.random.key(seed)
        ks = jax.random.split(key, 6)
        hidden_state = jax.random.normal(ks[0], (B, S, H), dtype=jnp.float32)
        adjacency_matrix = (jax.random.uniform(ks[1], (B, S, S)) < 0.2).astype(jnp.float32)
        W_left = 0.05 * jax.random.normal(ks[2], (L, H, H), dtype=jnp.float32)
        W_right = 0.05 * jax.random.normal(ks[3], (L, H, H), dtype=jnp.float32)
        W_lin = 0.05 * jax.random.normal(ks[4], (L, H, H), dtype=jnp.float32)
        b_lin = jnp.zeros((L, H), dtype=jnp.float32)
        ln_a = jnp.ones((L, H), dtype=jnp.float32)
        ln_b = jnp.zeros((L, H), dtype=jnp.float32)
        return {'hidden_state': hidden_state, 'adjacency_matrix': adjacency_matrix, 'W_left': W_left, 'W_right': W_right, 'W_lin': W_lin, 'b_lin': b_lin, 'ln_a': ln_a, 'ln_b': ln_b}
    _L0_gnn_all = _L0_gnn_setup()
    _L0_gnn_in = {k: v for k, v in _L0_gnn_all.items() if k in ('W_left', 'W_right', 'W_lin', 'b_lin', 'ln_a', 'ln_b', )}
    del _L0_gnn_all

    return {
        "x": x,
        "adj": adj,
        "L0_gnn_W_left": _L0_gnn_in["W_left"],
        "L0_gnn_W_right": _L0_gnn_in["W_right"],
        "L0_gnn_W_lin": _L0_gnn_in["W_lin"],
        "L0_gnn_b_lin": _L0_gnn_in["b_lin"],
        "L0_gnn_ln_a": _L0_gnn_in["ln_a"],
        "L0_gnn_ln_b": _L0_gnn_in["ln_b"],
    }

def reference(x, adj, L0_gnn_W_left, L0_gnn_W_right, L0_gnn_W_lin, L0_gnn_b_lin, L0_gnn_ln_a, L0_gnn_ln_b):
    import jax
    import jax.numpy as jnp
    def _L0_gnn_ref(hidden_state, adjacency_matrix, W_left, W_right, W_lin, b_lin, ln_a, ln_b):
        import jax, jax.numpy as jnp
        import numpy as np
        B, S, H, L = (32, 512, 768, 2)

        def _layer_norm(z, a, b, eps=0.001):
            mu = jnp.mean(z, axis=-1, keepdims=True)
            sigma = jnp.std(z, axis=-1, keepdims=True, ddof=1)
            return (z - mu) / (sigma + eps) * a + b
        temper = float(np.sqrt(H))
        adj = adjacency_matrix
        adj_tri = jnp.triu(adj, k=1)
        diag_mask = jnp.triu(adj, k=0) - adj_tri
        h = hidden_state
        for l in range(L):
            m_left = jnp.einsum('bsh,oh->bso', h, W_left[l])
            m_right = jnp.einsum('bsh,oh->bso', h, W_right[l])
            u_left = jnp.einsum('bih,bjh->bij', h, m_left) / temper
            u_right = jnp.einsum('bih,bjh->bij', h, m_right) / temper
            u = u_left * adj_tri + u_left * diag_mask + u_right * jnp.swapaxes(adj_tri, 1, 2)
            delta_exp_u = jnp.exp(u) * adj
            attention = delta_exp_u / (jnp.sum(delta_exp_u, axis=2, keepdims=True) + 1e-10)
            h_lin = jnp.einsum('bsh,oh->bso', h, W_lin[l]) + b_lin[l]
            ctx = jnp.matmul(attention, h_lin)
            h = jax.nn.relu(_layer_norm(ctx, ln_a[l], ln_b[l]))
        return h

    h = jnp.maximum(_layernorm(x, axis=-1), 0.0)
    x = x + _L0_gnn_ref(h, adj, L0_gnn_W_left, L0_gnn_W_right, L0_gnn_W_lin, L0_gnn_b_lin, L0_gnn_ln_a, L0_gnn_ln_b)
    return x


_drawn_inputs = setup_inputs


def setup_inputs(seed=0):
    import zlib

    import numpy as np

    out = dict(_drawn_inputs(seed))
    spreads = {'L0_gnn_b_lin': (0.0, 0.1), 'L0_gnn_ln_a': (1.0, 0.2), 'L0_gnn_ln_b': (0.0, 0.1)}
    factors = {}
    for name, (base, spread) in spreads.items():
        noise = np.random.default_rng([zlib.crc32(name.encode()), seed]).standard_normal(out[name].shape)
        drawn = base * np.exp(spread * noise) if base else spread * noise
        out[name] = jnp.asarray(drawn.astype(out[name].dtype))
    for name, factor in factors.items():
        out[name] = (out[name] * factor).astype(out[name].dtype)
    return out
```

```python
from contextlib import ExitStack

import concourse.bass as bass
from concourse import mybir

F32 = mybir.dt.float32
F32R = mybir.dt.float32r
BF16 = mybir.dt.bfloat16
ALU = mybir.AluOpType
ACT = mybir.ActivationFunctionType

HI, LO = 0, 1
LEFT, RIGHT, LIN = 0, 1, 2
PASSES = ((HI, HI), (LO, HI), (HI, LO))

M_BANKS = 4
C_BANKS = 2
TILES = 4
ET_ORDER = (0, 2, 1, 3)
H_SLOTS = (0, 1, 2, 0)
LOADED_BY = {0: (0, 3), 1: (1, 1), 2: (1, 2), 3: (1, 0)}


def m_phase_steps(extra, prepare=()):
    steps = []
    for part in range(2):
        for k in range(2):
            steps += [("M", k, 2 * part, 2 * part + 2, 0, 6), *extra.get((k, part), [])]
    for oc in range(1, 6):
        for k in (2 * oc, 2 * oc + 1):
            if (k, 0) in extra:
                steps += [("M", k, 0, 4, 0, 3), *extra[k, 0], ("M", k, 0, 4, 3, 6)]
            else:
                steps += [("M", k, 0, 4, 0, 6)]
            steps += extra.get((k, 1), [])
        steps += [("S", oc - 1)]
        if oc == 3:
            steps += [("X", t, 2) for t in prepare]
        if oc == 4:
            steps += [("N", t, 2) for t in prepare]
    return steps


def with_weights(extra, jobs):
    out = dict(extra)
    order = [(k, part) for part in range(2) for k in range(2)] + [(k, part) for k in range(2, 12) for part in range(2)]
    free = [key for key in order if not any(s[0] in "TCW" for s in extra.get(key, []))]
    for key, job in zip(free, jobs):
        out[key] = extra.get(key, []) + [("W", *job)]
    return out


def iteration_steps(has_next, norm_next, norm_after, weights_h=(), weights_m=()):
    w = [[("W", *n)] for n in weights_h] + [[]] * 3
    nxt = (lambda *s: list(s)) if has_next else (lambda *s: [])
    steps = [("H", 0, 0), *w[0], ("H", 0, 1), *w[1], ("S", 5), ("U", 0), ("U", 1), ("U", 2), ("U", 3),
             ("EM", 0), ("EM", 2), *nxt(("T", 0)), ("H", 1, 0), *w[2]]
    steps += [("X", 3, 1)] if norm_next else []
    steps += [("H", 1, 1), ("ET", 0), ("ET", 2), ("EM", 1), ("EM", 3), *nxt(("adj",), ("T", 1))]
    steps += [("N", 3, 1)] if norm_next else []
    steps += [("H", 2, 0), ("C", 0), ("ET", 1), ("ET", 3), ("H", 2, 1), *nxt(("T", 2)), ("F", 0),
              ("H", 3, 0), ("C", 1)]
    if not has_next:
        return steps + [("F", 1), ("H", 3, 1), ("C", 2), ("C", 3), ("F", 2), ("F", 3)]
    steps += [("H", 3, 1), ("T", 3), ("F", 1)]
    extra = {(0, 1): [("C", 2)], (1, 1): [("A",), ("F", 2)], (2, 1): [("C", 3)], (3, 1): [("F", 3)]}
    return steps + m_phase_steps(with_weights(extra, weights_m), (0, 1, 2) if norm_after else ())


def regions(groups):
    blocks = range(6)
    sides = [(m, b) for b in blocks for m in (LEFT, RIGHT)]
    lins = [(LIN, b) for b in blocks]
    start = [("W", *sides[0]), ("X", 0, 1), ("X", 1, 1), ("X", 2, 1), ("N", 0, 1), ("N", 1, 1), ("N", 2, 1),
             ("T", 0), ("W", *sides[1]), ("T", 1), ("A",)]
    extra = {(0, 0): [("T", 2), ("X", 3, 1), ("N", 3, 1)], (1, 0): [("T", 3)]}
    parts = [(-1, 0, False, start + m_phase_steps(with_weights(extra, sides[2:] + lins), (0, 1, 2)))]
    half = groups // 2
    steady0 = iteration_steps(True, True, True)
    parts.append((0, 1, False, steady0))
    parts.append((1, half - 2, True, steady0))
    parts.append((half - 2, half - 1, False, iteration_steps(True, True, False)))
    parts.append((half - 1, half, False, iteration_steps(True, False, False, sides[:3], sides[3:] + lins)))
    parts.append((half, groups - 2, True, iteration_steps(True, False, False)))
    parts.append((groups - 2, groups - 1, False, iteration_steps(True, False, False)))
    parts.append((groups - 1, groups, False, iteration_steps(False, False, False)))
    out, at = [], 0
    for first, end, looped, steps in parts:
        jobs = [s for s in steps if s[0] in "TCW"]
        out.append((first, end, looped, steps, at, len(jobs)))
        at += len(jobs) * (end - first)
    return out


def gnn_kernel(nc, x, adj, w_left, w_right, w_lin, b_lin, ln_a, ln_b, h1, out):
    B, S, _ = adj.shape
    H = x.shape[2]
    L = w_left.shape[0]
    P = 128
    KC = H // P
    HALF = H // 2
    HC = KC // 2
    ROWS = TILES * P
    PER = B * S // ROWS
    GROUPS = L * PER
    M_JOBS = 2 * KC + 2 * TILES
    H_JOB = 2 * KC
    W_JOBS = 3 * KC
    INV_TEMPER = 1.0 / float(H) ** 0.5
    DDOF = H / (H - 1.0)
    EPS_STD, EPS_SUM, EPS_LN = 1e-3, 1e-10, 1e-5
    assert 2 * S == P and H == 2 * HALF and L == 2 and TILES == 4 and KC == 6
    PARTS = regions(GROUPS)
    weights = (w_left, w_right, w_lin)

    x_rows = x.rearrange("b s h -> (b s) h")
    out_rows = out.rearrange("b s h -> (b s) h")
    adj_group = adj.rearrange("(g t b) i j -> g (b i) t j", g=PER, t=TILES)

    with ExitStack() as ctx:
        def sb(name, shape, dt):
            return ctx.enter_context(nc.sbuf_tensor(name, shape, dt))

        def sem(name):
            return ctx.enter_context(nc.semaphore(name))

        wt = sb("wt", [P, 3, 2, KC, H], F32R)
        ht = sb("ht", [P, 2, KC, ROWS], F32R)
        mt = sb("mt", [P, 2, 2, 2, ROWS], F32R)
        hl = sb("hl", [P, 3, 2, H], F32R)
        rows = sb("rows", [P, 3, H], F32)
        side = sb("side", [P, 4, H], F32)
        vec = sb("vec", [P, 3, H], F32)
        ebd = sb("ebd", [P, 2, P], F32)
        et = sb("et", [P, TILES, 2, P], F32R)
        mask = sb("mask", [P, TILES, 2, S], F32)
        adj2 = sb("adj2", [P, TILES, 2, S], F32)
        um = sb("um", [P, 2, S], F32)
        us = sb("us", [P, TILES, S], F32)
        ident = sb("ident", [P, P], F32)
        upper = sb("upper", [P, S], BF16)
        lower = sb("lower", [P, S], BF16)
        powers = sb("powers", [P, 2], F32)
        stats = sb("stats", [P, 2, 6], F32)
        xstats = sb("xstats", [P, 2, 6], F32)
        mom = sb("mom", [P, TILES, 2], F32)
        xmom = sb("xmom", [P, TILES, 2], F32)
        col = sb("col", [P, 9, TILES], F32)
        ESUM, VAR, STD, FLOOR, DEN, SCALE, XVAR, XRSTD, XSHIFT = range(9)

        pm = ctx.enter_context(nc.psum_tensor("pm", [P, M_BANKS, 512], F32))
        pu = ctx.enter_context(nc.psum_tensor("pu", [P, TILES, 2 * P], F32))
        pc = ctx.enter_context(nc.psum_tensor("pc", [P, C_BANKS, 512], F32))

        const_base = sem("const_base")
        const_ready = sem("const_ready")
        vec_loaded = sem("vec_loaded")
        adj_loaded = sem("adj_loaded")
        x_loaded = [sem(f"x_loaded{i}") for i in range(3)]
        res_loaded = [sem(f"res_loaded{i}") for i in range(2)]
        w_loaded = [sem(f"w_loaded{i}") for i in range(4)]
        stored = [sem(f"stored{i}") for i in range(2)]
        m_full = sem("m_full")
        m_hi = sem("m_hi")
        m_clear = sem("m_clear")
        c_full = sem("c_full")
        ht_hi = sem("ht_hi")
        w_hi = sem("w_hi")
        c_clear = sem("c_clear")
        u_full = sem("u_full")
        u_masked = sem("u_masked")
        u_summed = sem("u_summed")
        e_exp = sem("e_exp")
        e_masked = sem("e_masked")
        et_full = sem("et_full")
        et_hi = sem("et_hi")
        et_clear = sem("et_clear")
        a_full = sem("a_full")
        mask_ready = sem("mask_ready")
        c_stats = sem("c_stats")
        c_moments = sem("c_moments")
        c_var = sem("c_var")
        c_floor = sem("c_floor")
        c_std = sem("c_std")
        c_den = sem("c_den")
        c_scale = sem("c_scale")
        f_centred = sem("f_centred")
        f_affine = sem("f_affine")
        f_done = sem("f_done")
        x_stats = sem("x_stats")
        x_moments = sem("x_moments")
        x_eps = sem("x_eps")
        x_var = sem("x_var")
        x_rstd = sem("x_rstd")
        x_shift = sem("x_shift")
        x_norm = sem("x_norm")

        def ring_after(part, G, step, halves=2):
            first, _, _, steps, at, grow = part
            jobs = [s for s in steps if s[0] in "TCW"]
            return 2 * grow * (G - first) + 2 * (at + jobs.index(step)) + halves

        def tile_count(G, n, per=1):
            return 4 * per * G + per * n

        def x_load_count(G, t):
            return 32 * G + (32 if t == 3 else 16) if t in (0, 3) else 16 * G + 16

        def w_slot(G, step):
            order = [s for p in PARTS for s in p[3] if s[0] == "W"]
            layer = 0 if G < 0 else 1
            i = order.index(step, W_JOBS * layer)
            if layer == 0:
                return i, i % 4, 16 * (i // 4 + 1)
            i1 = i - W_JOBS
            used = len(range(2 + i1 % 2, W_JOBS, 4))
            return i, 2 + i1 % 2, 16 * (used + i1 // 2 + 1)

        def wait_from(engine, semaphore, value):
            if isinstance(value, int) and value <= 0:
                return
            engine.wait_ge(semaphore, value)

        def each_part(engine, walk):
            for part in PARTS:
                first, end, looped = part[:3]
                if looped:
                    with engine.Fori(first, end) as G:
                        walk(part, G)
                else:
                    walk(part, first)

        def w_order():
            return [s for p in PARTS for s in p[3] if s[0] == "W"]

        block = ctx.enter_context(nc.Block())

        @block.sync
        def _(sp):
            order = w_order()

            def load_weights(i):
                layer = i // W_JOBS
                _, mat, ob = order[i]
                slot = i % 4 if layer == 0 else 2 + (i - W_JOBS) % 2
                sp.dma_start(side[:, slot, :], weights[mat][layer, ob * P:(ob + 1) * P, :]).then_inc(w_loaded[slot], 16)

            def load_vectors(layer):
                for i, v in enumerate((b_lin, ln_a, ln_b)):
                    sp.dma_start(vec[:, i, :], v[layer:layer + 1, :].to_broadcast([P, H])).then_inc(vec_loaded, 16)

            def load_adjacency(g):
                for twin in range(2):
                    sp.dma_start(adj2[:, :, twin, :], adj_group[g]).then_inc(adj_loaded, 16)

            def load_rows(source, g, t):
                sp.dma_start(rows[:, H_SLOTS[t], :], source[bass.ds((g * TILES + t) * P, P), :]).then_inc(
                    x_loaded[H_SLOTS[t]], 16)

            def load_residual(row_tile, t):
                sp.dma_start(side[:, 2 + t % 2, :], x_rows[bass.ds(row_tile * P, P), :]).then_inc(res_loaded[t % 2], 16)

            for t in range(3):
                load_rows(x_rows, 0, t)
                if t < 2:
                    load_weights(t)
            load_weights(2)
            load_adjacency(0)
            load_weights(3)
            load_vectors(0)

            def walk(part, G):
                first, end, looped, steps, _, _ = part
                layer = 1 if first >= PER else 0
                g = G - PER * layer
                for step in steps:
                    kind = step[0]
                    if kind == "T":
                        on, t = LOADED_BY[step[1]]
                        g2_first = first + 1 + on
                        if g2_first < GROUPS:
                            sp.wait_ge(c_full, ring_after(part, G, step))
                            if g2_first < PER:
                                load_rows(x_rows, G + 1 + on, t)
                            else:
                                g2 = G + 1 + on - PER
                                if first < PER:
                                    sp.wait_ge(stored[t % 2], 32 * g2 + 16 * (t // 2) + 16)
                                load_rows(h1, g2, t)
                    if kind == "adj":
                        sp.wait_ge(e_masked, tile_count(G, 4, 2))
                        nxt = 0 if first == PER - 1 else g + 1
                        load_adjacency(nxt)
                    if kind == "W":
                        i, _, _ = w_slot(first, step)
                        last = (i < W_JOBS) and i + 4 < W_JOBS or i >= W_JOBS and i + 2 < 2 * W_JOBS
                        if last:
                            sp.wait_ge(c_full, ring_after(part, G, step))
                            load_weights(i + (4 if i < W_JOBS else 2))
                        elif i >= 2 * W_JOBS - 2:
                            sp.wait_ge(c_full, ring_after(part, G, step))
                            t = (i - 2 * W_JOBS) % 2
                            load_residual(t, t)
                    if kind == "F":
                        t = step[1]
                        dest = out_rows if layer else h1
                        sp.wait_ge(f_done, tile_count(G, t + 1))
                        sp.dma_start(dest[bass.ds((g * TILES + t) * P, P), :], side[:, t % 2, :]).then_inc(stored[t % 2], 16)
                        if layer and (first < GROUPS - 1 or t < 2):
                            load_residual(g * TILES + t + 2, t)
                        if first == PER - 1 and t == 3:
                            load_vectors(1)
                    if first == PER - 2 and step == ("N", 3, 1):
                        for i in range(W_JOBS, W_JOBS + 2):
                            load_weights(i)
                if first == PER - 1:
                    for t in range(2):
                        sp.wait_ge(stored[t], 32 * PER)

            each_part(sp, walk)
            for t in range(2):
                sp.wait_ge(stored[t], 16 * 2 * GROUPS)

        @block.gpsimd
        def _(pool):
            nc.gpsimd.memset(ident[:], 0.0).then_inc(const_base, 1)
            nc.gpsimd.memset(upper[:], 1.0).then_inc(const_base, 1)
            nc.gpsimd.memset(lower[:], 1.0).then_inc(const_base, 1)
            nc.gpsimd.memset(ebd[:], 0.0).then_inc(const_ready, 1)
            nc.gpsimd.memset(powers[:, 0:1], 0.5).then_inc(const_ready, 1)
            nc.gpsimd.memset(powers[:, 1:2], -0.5).then_inc(const_ready, 1)
            pool.wait_ge(const_base, 3)
            pool.wait_ge(const_ready, 3)
            nc.gpsimd.affine_select(out=ident[:], in_=ident[:], compare_op=ALU.not_equal, fill=1.0, base=0,
                                    pattern=[[1, P]], channel_multiplier=-1).then_inc(const_ready, 1)
            for b in range(2):
                own = slice(b * S, (b + 1) * S)
                pool.wait_ge(const_ready, 4 + 2 * b)
                nc.gpsimd.affine_select(out=upper[own, :], in_=upper[own, :], compare_op=ALU.is_ge, fill=0.0, base=0,
                                        pattern=[[1, S]], channel_multiplier=-1).then_inc(const_ready, 1)
                pool.wait_ge(const_ready, 5 + 2 * b)
                nc.gpsimd.affine_select(out=lower[own, :], in_=lower[own, :], compare_op=ALU.is_gt, fill=0.0, base=0,
                                        pattern=[[-1, S]], channel_multiplier=1).then_inc(const_ready, 1)
            pool.wait_ge(const_ready, 8)

            def walk(part, G):
                first, end, looped, steps, _, _ = part
                for step in steps:
                    kind = step[0]
                    if kind == "C":
                        t = step[1]
                        pool.wait_ge(c_var, tile_count(G, t + 1))
                        nc.gpsimd.tensor_tensor(col[:, STD, t:t + 1], col[:, VAR, t:t + 1], powers[:, 0:1],
                                                ALU.pow).then_inc(c_std, 1)
                    if kind == "X":
                        t = step[1]
                        pool.wait_ge(x_var, tile_count(G + step[2], t + 1))
                        nc.gpsimd.tensor_tensor(col[:, XRSTD, t:t + 1], col[:, XVAR, t:t + 1], powers[:, 1:2],
                                                ALU.pow).then_inc(x_rstd, 1)

            each_part(pool, walk)

        @block.tensor
        def _(pe):
            pe.wait_ge(const_ready, 8)

            def transposes(part, G, step, source):
                for half in range(2):
                    pe.wait_ge(c_clear, ring_after(part, G, step, half - 1) + C_BANKS)
                    for j in range(HC):
                        kc = half * HC + j
                        last = nc.tensor.transpose(pc[:, half, j * P:(j + 1) * P], source[:, kc * P:(kc + 1) * P], ident[:])
                    last.then_inc(c_full, 1)

            def project(k, t0, t1, c0, c1):
                oc, lr = k // 2, k % 2
                own = slice(t0 * P, t1 * P)
                for kc in range(c0, c1):
                    for n, (a, b) in enumerate(PASSES):
                        last = nc.tensor.matmul(pm[:, k % M_BANKS, own], wt[:, lr, a, kc, oc * P:(oc + 1) * P],
                                                ht[:, b, kc, own], start=(kc == 0 and n == 0),
                                                stop=(kc == KC - 1 and n == len(PASSES) - 1))
                return last

            def walk(part, G):
                first, end, looped, steps, _, _ = part
                N = G + 1
                fresh = first in (-1, PER - 1)
                for step in steps:
                    kind = step[0]
                    if kind == "T":
                        t = step[1]
                        if first + 1 < PER:
                            pe.wait_ge(x_norm, tile_count(N, t + 1))
                        else:
                            pe.wait_ge(x_loaded[H_SLOTS[t]], x_load_count(N, t))
                        transposes(part, G, step, rows[:, H_SLOTS[t], :])
                    elif kind == "W":
                        _, slot, count = w_slot(first, step)
                        pe.wait_ge(w_loaded[slot], count)
                        transposes(part, G, step, side[:, slot, :])
                    elif kind == "M":
                        k, t0, t1, c0, c1 = step[1:]
                        if t0 == 0 and c0 == 0:
                            pe.wait_ge(m_clear, M_JOBS * N + k - M_BANKS + 1 + M_BANKS)
                            if fresh:
                                pe.wait_ge(c_clear, ring_after(part, G, ("W", k % 2, k // 2)) + C_BANKS)
                        if k < 2:
                            pe.wait_ge(c_clear, ring_after(part, G, ("T", t1 - 1)) + C_BANKS)
                        last = project(*step[1:])
                        if t1 == TILES and c1 == KC:
                            last.then_inc(m_full, 1)
                    elif kind == "S":
                        oc = step[1]
                        Q = G if oc == KC - 1 else N
                        pe.wait_ge(m_clear, M_JOBS * Q + 2 * oc + 2 + M_BANKS)
                        if oc == 0:
                            pe.wait_ge(mask_ready, 3 * N + 3)
                        for t in range(TILES):
                            for n, (a, b) in enumerate(PASSES):
                                last = nc.tensor.matmul(
                                    pu[:, t, :], ht[:, a, oc, t * P:(t + 1) * P],
                                    mt[:, oc % 2, b, :, t * P:(t + 1) * P],
                                    start=(oc == 0 and n == 0 and t % 2 == 0),
                                    stop=(oc == KC - 1 and n == 2), skip_group_check=True)
                            if oc == KC - 1 and t % 2 == 1:
                                last.then_inc(u_full, 1)
                    elif kind == "H":
                        t, half = step[1:]
                        j = H_JOB + 2 * t + half
                        pe.wait_ge(m_clear, M_JOBS * G + j - M_BANKS + 1 + M_BANKS)
                        n = 0
                        for kc in range(KC):
                            for a, b in PASSES:
                                last = nc.tensor.matmul(
                                    pm[:, j % M_BANKS, 0:HALF], ht[:, a, kc, t * P:(t + 1) * P],
                                    wt[:, LIN, b, kc, half * HALF:(half + 1) * HALF],
                                    start=(n == 0), stop=(n == 3 * KC - 1))
                                n += 1
                        last.then_inc(m_full, 1)
                    elif kind == "ET":
                        t = step[1]
                        p = ET_ORDER.index(t)
                        pe.wait_ge(e_masked, tile_count(G, p + 1, 2))
                        if p >= 2:
                            pe.wait_ge(et_clear, tile_count(G, p - 1))
                        nc.tensor.transpose(pu[:, t, 0:P], ebd[:, t // 2, :], ident[:]).then_inc(et_full, 1)
                    elif kind == "A":
                        pe.wait_ge(adj_loaded, 32 * N + 32)
                        wait_from(pe, et_clear, tile_count(N, 0))
                        for t in range(TILES):
                            last = nc.tensor.transpose(pu[:, t, 0:P], adj2[:, t, :, :].rearrange("p a b -> p (a b)"), ident[:])
                        last.then_inc(a_full, 1)
                    elif kind == "C":
                        t = step[1]
                        pe.wait_ge(et_clear, tile_count(G, ET_ORDER.index(t) + 1))
                        pe.wait_ge(m_clear, M_JOBS * G + H_JOB + 2 * t + 2 + M_BANKS)
                        for half in range(2):
                            pe.wait_ge(c_clear, ring_after(part, G, step, half - 1) + C_BANKS)
                            for n, (a, b) in enumerate(PASSES):
                                last = nc.tensor.matmul(
                                    pc[:, half, 0:HALF], et[:, t, a, :],
                                    hl[:, H_SLOTS[t], b, half * HALF:(half + 1) * HALF], start=(n == 0), stop=(n == 2))
                            last.then_inc(c_full, 1)
                if fresh:
                    pe.wait_ge(c_clear, ring_after(part, G, [s for s in steps if s[0] == "W"][-1]) + C_BANKS)

            each_part(pe, walk)

        @block.scalar
        def _(act):
            def walk(part, G):
                first, end, looped, steps, _, _ = part
                N = G + 1
                layer = 1 if first >= PER else 0
                for step in steps:
                    kind = step[0]
                    if kind in ("T", "W"):
                        for half in range(2):
                            act.wait_ge(c_full, ring_after(part, G, step, half + 1))
                            src = pc[:, half, 0:HALF].rearrange("p (c n) -> p c n", c=HC)
                            if kind == "T":
                                t = step[1]
                                dst = ht[:, HI, half * HC:(half + 1) * HC, t * P:(t + 1) * P]
                                nc.scalar.copy(dst, src).then_inc(ht_hi, 1)
                            else:
                                mat, ob = step[1:]
                                dst = wt[:, mat, HI, half * HC:(half + 1) * HC, ob * P:(ob + 1) * P]
                                nc.scalar.copy(dst, src).then_inc(w_hi, 1)
                    elif kind == "M" and step[3] == TILES and step[5] == KC:
                        k = step[1]
                        act.wait_ge(m_full, M_JOBS * N + k + 1)
                        nc.scalar.copy(mt[:, k // 2 % 2, HI, k % 2, :], pm[:, k % M_BANKS, :]).then_inc(m_hi, 1)
                    elif kind == "H":
                        t, half = step[1:]
                        j = H_JOB + 2 * t + half
                        act.wait_ge(m_full, M_JOBS * G + j + 1)
                        nc.scalar.copy(hl[:, H_SLOTS[t], HI, half * HALF:(half + 1) * HALF],
                                       pm[:, j % M_BANKS, 0:HALF]).then_inc(m_hi, 1)
                    elif kind == "U":
                        t = step[1]
                        act.wait_ge(u_summed, tile_count(G, t + 1))
                        nc.scalar.activation(us[:, t, :], us[:, t, :], ACT.Exp, scale=INV_TEMPER).then_inc(e_exp, 1)
                    elif kind == "ET":
                        t = step[1]
                        act.wait_ge(et_full, tile_count(G, ET_ORDER.index(t) + 1))
                        nc.scalar.copy(et[:, t, HI, :], pu[:, t, 0:P]).then_inc(et_hi, 1)
                    elif kind == "N":
                        t = step[1]
                        act.wait_ge(x_shift, tile_count(G + step[2], t + 1))
                        row = rows[:, H_SLOTS[t], :]
                        nc.scalar.activation(row, row, ACT.Relu, bias=col[:, XSHIFT, t:t + 1],
                                             scale=col[:, XRSTD, t:t + 1]).then_inc(x_norm, 1)
                    elif kind == "F" and layer == 0:
                        t = step[1]
                        act.wait_ge(f_affine, tile_count(G, t + 1))
                        nc.scalar.activation(side[:, t % 2, :], side[:, t % 2, :], ACT.Relu).then_inc(f_done, 1)

            each_part(act, walk)

        @block.vector
        def _(dve):
            nc.vector.memset(um[:, 0, 0:1], 0.0).then_inc(m_clear, M_BANKS)
            nc.vector.memset(um[:, 1, 0:1], 0.0).then_inc(c_clear, C_BANKS)
            dve.wait_ge(const_ready, 8)

            def low_part(dst, src, hi):
                return nc.vector.tensor_tensor(dst, src, hi.bitcast(F32), ALU.subtract)

            def walk(part, G):
                first, end, looped, steps, _, _ = part
                N = G + 1
                layer = 1 if first >= PER else 0
                for step in steps:
                    kind = step[0]
                    if kind in ("T", "W"):
                        for half in range(2):
                            src = pc[:, half, 0:HALF].rearrange("p (c n) -> p c n", c=HC)
                            if kind == "T":
                                t = step[1]
                                dve.wait_ge(ht_hi, tile_count(N, t, 2) + half + 1)
                                at = (slice(half * HC, (half + 1) * HC), slice(t * P, (t + 1) * P))
                                op = low_part(ht[:, LO, at[0], at[1]], src, ht[:, HI, at[0], at[1]])
                            else:
                                mat, ob = step[1:]
                                dve.wait_ge(w_hi, 2 * w_slot(first, step)[0] + half + 1)
                                at = (slice(half * HC, (half + 1) * HC), slice(ob * P, (ob + 1) * P))
                                op = low_part(wt[:, mat, LO, at[0], at[1]], src, wt[:, mat, HI, at[0], at[1]])
                            op.then_inc(c_clear, 1)
                    elif kind == "M" and step[3] == TILES and step[5] == KC:
                        k = step[1]
                        dve.wait_ge(m_hi, M_JOBS * N + k + 1)
                        low_part(mt[:, k // 2 % 2, LO, k % 2, :], pm[:, k % M_BANKS, :],
                                 mt[:, k // 2 % 2, HI, k % 2, :]).then_inc(m_clear, 1)
                    elif kind == "H":
                        t, half = step[1:]
                        j = H_JOB + 2 * t + half
                        dve.wait_ge(m_hi, M_JOBS * G + j + 1)
                        at = slice(half * HALF, (half + 1) * HALF)
                        low_part(hl[:, H_SLOTS[t], LO, at], pm[:, j % M_BANKS, 0:HALF],
                                 hl[:, H_SLOTS[t], HI, at]).then_inc(m_clear, 1)
                    elif kind == "A":
                        dve.wait_ge(a_full, N + 1)
                        nc.vector.tensor_tensor(mask[:, :, 0, :], adj2[:, :, 0, :],
                                                upper[:].unsqueeze(1).to_broadcast([P, TILES, S]),
                                                ALU.mult).then_inc(mask_ready, 1)
                        for b in range(2):
                            own = slice(b * S, (b + 1) * S)
                            nc.vector.tensor_tensor(mask[own, :, 1, :], pu[own, :, own],
                                                    lower[own, :].unsqueeze(1).to_broadcast([S, TILES, S]),
                                                    ALU.mult).then_inc(mask_ready, 1)
                    elif kind == "U":
                        t = step[1]
                        dve.wait_ge(u_full, 2 * G + t // 2 + 1)
                        if t == 0:
                            dve.wait_ge(mask_ready, 3 * G + 3)
                        wait_from(dve, u_summed, tile_count(G, t))
                        scores = pu[:, t, :].rearrange("p (m j) -> p m j", m=2)
                        for b in range(2):
                            own = slice(b * S, (b + 1) * S)
                            nc.vector.tensor_tensor(um[own, :, :], scores[own, :, own], mask[own, t, :, :],
                                                    ALU.mult).then_inc(u_masked, 1)
                        dve.wait_ge(u_masked, tile_count(G, t + 1, 2))
                        nc.vector.tensor_tensor(us[:, t, :], um[:, 0, :], um[:, 1, :], ALU.add).then_inc(u_summed, 1)
                    elif kind == "EM":
                        t = step[1]
                        p = ET_ORDER.index(t)
                        dve.wait_ge(e_exp, tile_count(G, t + 1))
                        if p >= 2:
                            dve.wait_ge(et_full, tile_count(G, p - 1))
                        for b in range(2):
                            own = slice(b * S, (b + 1) * S)
                            nc.vector.tensor_tensor_reduce(
                                out=ebd[own, t // 2, own], in0=us[own, t, :], in1=adj2[own, t, 0, :], scale=1.0,
                                scalar=0.0, op0=ALU.mult, op1=ALU.add,
                                accum_out=col[own, ESUM, t:t + 1]).then_inc(e_masked, 1)
                    elif kind == "ET":
                        t = step[1]
                        dve.wait_ge(et_hi, tile_count(G, ET_ORDER.index(t) + 1))
                        low_part(et[:, t, LO, :], pu[:, t, 0:P], et[:, t, HI, :]).then_inc(et_clear, 1)
                    elif kind == "C":
                        t = step[1]
                        if t == 0:
                            dve.wait_ge(vec_loaded, 48 * (layer + 1))
                        wait_from(dve, stored[t % 2], 32 * G + 16 * (t // 2))
                        dve.wait_ge(e_masked, tile_count(G, ET_ORDER.index(t) + 1, 2))
                        for half in range(2):
                            at = slice(half * HALF, (half + 1) * HALF)
                            dve.wait_ge(c_full, ring_after(part, G, step, half + 1))
                            nc.vector.scalar_tensor_tensor(
                                out=side[:, t % 2, at], in0=vec[:, 0, at], scalar=col[:, ESUM, t:t + 1],
                                in1=pc[:, half, 0:HALF], op0=ALU.mult, op1=ALU.add).then_inc(c_clear, 1)
                        wait_from(dve, c_moments, tile_count(G, t))
                        for half in range(2):
                            dve.wait_ge(c_clear, ring_after(part, G, step, half + 1) + C_BANKS)
                            nc.vector.bn_stats(stats[:, half, :], side[:, t % 2, half * HALF:(half + 1) * HALF]
                                               ).then_inc(c_stats, 1)
                        dve.wait_ge(c_stats, tile_count(G, t + 1, 2))
                        nc.vector.tensor_scalar(col[:, FLOOR, t:t + 1], col[:, ESUM, t:t + 1], EPS_SUM, EPS_STD,
                                                ALU.add, ALU.mult).then_inc(c_floor, 1)
                        nc.vector.bn_aggr(mom[:, t, :], stats[:].rearrange("p a b -> p (a b)")).then_inc(c_moments, 1)
                        dve.wait_ge(c_moments, tile_count(G, t + 1))
                        nc.vector.tensor_scalar(col[:, VAR, t:t + 1], mom[:, t, 1:2], DDOF, None,
                                                ALU.mult).then_inc(c_var, 1)
                    elif kind == "F":
                        t = step[1]
                        n = tile_count(G, t + 1)
                        row = side[:, t % 2, :]
                        nc.vector.scalar_tensor_tensor(out=row, in0=row, scalar=mom[:, t, 0:1], in1=vec[:, 1, :],
                                                       op0=ALU.subtract, op1=ALU.mult).then_inc(f_centred, 1)
                        dve.wait_ge(c_std, n)
                        dve.wait_ge(c_floor, n)
                        nc.vector.tensor_tensor(col[:, DEN, t:t + 1], col[:, STD, t:t + 1], col[:, FLOOR, t:t + 1],
                                                ALU.add).then_inc(c_den, 1)
                        dve.wait_ge(c_den, n)
                        nc.vector.reciprocal(col[:, SCALE, t:t + 1], col[:, DEN, t:t + 1]).then_inc(c_scale, 1)
                        dve.wait_ge(c_scale, n)
                        dve.wait_ge(f_centred, n)
                        nc.vector.scalar_tensor_tensor(out=row, in0=row, scalar=col[:, SCALE, t:t + 1],
                                                       in1=vec[:, 2, :], op0=ALU.mult, op1=ALU.add).then_inc(f_affine, 1)
                        if layer:
                            dve.wait_ge(f_affine, n)
                            dve.wait_ge(res_loaded[t % 2], 32 * (G - PER) + 16 * (t // 2) + 16)
                            nc.vector.scalar_tensor_tensor(out=row, in0=row, scalar=0.0, in1=side[:, 2 + t % 2, :],
                                                           op0=ALU.max, op1=ALU.add).then_inc(f_done, 1)
                    elif kind == "X":
                        t = step[1]
                        X = G + step[2]
                        dve.wait_ge(x_loaded[H_SLOTS[t]], x_load_count(X, t))
                        wait_from(dve, x_moments, tile_count(X, t))
                        for half in range(2):
                            nc.vector.bn_stats(xstats[:, half, :],
                                               rows[:, H_SLOTS[t], half * HALF:(half + 1) * HALF]).then_inc(x_stats, 1)
                        dve.wait_ge(x_stats, tile_count(X, t + 1, 2))
                        nc.vector.memset(col[:, XVAR, t:t + 1], EPS_LN).then_inc(x_eps, 1)
                        nc.vector.bn_aggr(xmom[:, t, :], xstats[:].rearrange("p a b -> p (a b)")).then_inc(x_moments, 1)
                        dve.wait_ge(x_moments, tile_count(X, t + 1))
                        dve.wait_ge(x_eps, tile_count(X, t + 1))
                        nc.vector.tensor_tensor(col[:, XVAR, t:t + 1], xmom[:, t, 1:2], col[:, XVAR, t:t + 1],
                                                ALU.add).then_inc(x_var, 1)
                    elif kind == "N":
                        t = step[1]
                        X = G + step[2]
                        dve.wait_ge(x_rstd, tile_count(X, t + 1))
                        nc.vector.scalar_tensor_tensor(out=col[:, XSHIFT, t:t + 1], in0=xmom[:, t, 0:1], scalar=-1.0,
                                                       in1=col[:, XRSTD, t:t + 1], op0=ALU.mult,
                                                       op1=ALU.mult).then_inc(x_shift, 1)

            each_part(dve, walk)


_INS = ["x", "adj", "L0_gnn_W_left", "L0_gnn_W_right", "L0_gnn_W_lin", "L0_gnn_b_lin", "L0_gnn_ln_a", "L0_gnn_ln_b"]


def kernel(**inputs):
    import numpy as _np
    import concourse.bacc as _bacc
    from concourse import mybir as _mybir
    from concourse.bass_utils import run_bass_kernel_spmd as _run

    nc = _bacc.Bacc("TRN2", target_bir_lowering=False, num_devices=1)
    arrays, args = {}, []
    for name in _INS:
        a = _np.ascontiguousarray(inputs[name])
        arrays[f"in_{name}_dram"] = a
        args.append(nc.dram_tensor(f"in_{name}_dram", a.shape, _mybir.dt.from_np(a.dtype), kind="ExternalInput").ap())
    shape = inputs["x"].shape
    h1 = nc.dram_tensor("h1_dram", (shape[0] * shape[1], shape[2]), _mybir.dt.float32, kind="Internal").ap()
    out = nc.dram_tensor("out_0_dram", shape, _mybir.dt.float32, kind="ExternalOutput").ap()
    gnn_kernel(nc, *args, h1, out)
    r = _run(nc, [arrays], core_ids=[0])
    return r.results[0]["out_0_dram"]
```

```python
from contextlib import ExitStack

import concourse.bass as bass
from concourse import mybir

F32 = mybir.dt.float32
F32R = mybir.dt.float32r
BF16 = mybir.dt.bfloat16
ALU = mybir.AluOpType
ACT = mybir.ActivationFunctionType

HI, LO = 0, 1
LEFT, RIGHT, LIN = 0, 1, 2
ML, ADJ, MR = 0, 1, 2
PASSES = ((HI, HI), (LO, HI), (HI, LO))

M_BANKS = 2
C_BANKS = 2
TILES = 4
H_SLOTS = (0, 1, 2, 0)
LOADED_BY = {0: (0, 3), 1: (1, 1), 2: (1, 2), 3: (1, 0)}


def m_parts(lead):
    order = [(k, part) for k0 in range(0, lead, 4) for part in range(2) for k in range(k0, min(k0 + 4, lead))]
    return order + [(k, part) for k in range(lead, 12) for part in range(2)]


def m_phase_steps(extra, lead, prepare=()):
    steps = []
    for k, part in m_parts(lead):
        if k < lead:
            steps += [("M", k, 2 * part, 2 * part + 2, 0, 6)]
        elif (k, 0) in extra:
            steps += [("M", k, 0, 4, 3 * part, 3 * part + 3)]
        elif part == 1:
            steps += [("M", k, 0, 4, 0, 6)]
        steps += extra.get((k, part), [])
        oc = k // 2
        if k % 2 == 1 and part == 1 and oc > 0:
            steps += [("S", oc - 1)]
            if oc == 3:
                steps += [("X", t, 2) for t in prepare]
            if oc == 4:
                steps += [("N", t, 2) for t in prepare]
    return steps


def with_weights(extra, lead, jobs):
    out = dict(extra)
    free = [key for key in m_parts(lead) if not any(s[0] in "TCW" for s in extra.get(key, []))]
    for key, job in zip(free, jobs):
        out[key] = [("W", *job)] + extra.get(key, [])
    return out


def iteration_steps(has_next, norm_next, norm_after, weights_h=(), weights_m=()):
    w = [[("W", *n)] for n in weights_h] + [[]] * 3
    nxt = (lambda *s: list(s)) if has_next else (lambda *s: [])
    steps = [("H", 0, 0), *w[0], ("H", 0, 1), ("S", 5), ("U", 0), ("U", 1), ("EX", 0), ("H", 1, 0), *nxt(("T", 0)),
             ("EM", 0), ("EX", 1), ("H", 1, 1), *w[1], ("EM", 1), *nxt(("adj",)), ("H", 2, 0), *w[2], ("ET", 0), ("ET", 1),
             *nxt(("T", 1)), *nxt(*[("X", 3, 1)] * norm_next), ("H", 2, 1), ("C", 0)]
    if not has_next:
        return steps + [("H", 3, 0), ("C", 1), ("F", 0), ("H", 3, 1), ("C", 2), ("F", 1), ("C", 3), ("F", 2), ("F", 3)]
    steps += [("H", 3, 0), ("T", 2)] + ([("N", 3, 1)] if norm_next else []) + [("H", 3, 1), ("T", 3)]
    extra = {(0, 1): [("C", 1)], (1, 1): [("A",), ("F", 0)], (3, 1): [("C", 2)], (4, 1): [("F", 1)],
             (6, 1): [("C", 3)], (7, 1): [("F", 2)], (8, 1): [("F", 3)]}
    return steps + m_phase_steps(with_weights(extra, 2, weights_m), 2, (0, 1, 2) if norm_after else ())


def regions(groups):
    blocks = range(6)
    sides = [(m, b) for b in blocks for m in (LEFT, RIGHT)]
    lins = [(LIN, b) for b in blocks]
    start = [("X", 0, 1), ("N", 0, 1), ("X", 1, 1), ("N", 1, 1), ("T", 0), ("W", *sides[0]), ("T", 1), ("W", *sides[1]),
             ("X", 2, 1), ("N", 2, 1)]
    extra = {(0, 0): [("T", 2), ("X", 3, 1), ("N", 3, 1)], (1, 0): [("T", 3)], (1, 1): [("A",)]}
    parts = [(-1, 0, False, start + m_phase_steps(with_weights(extra, 2, sides[2:] + lins), 2, (0, 1, 2)))]
    half = groups // 2
    steady0 = iteration_steps(True, True, True)
    parts.append((0, 1, False, steady0))
    parts.append((1, half - 2, True, steady0))
    parts.append((half - 2, half - 1, False, iteration_steps(True, True, False)))
    parts.append((half - 1, half, False, iteration_steps(True, False, False, sides[:3], sides[3:] + lins)))
    parts.append((half, groups - 2, True, iteration_steps(True, False, False)))
    parts.append((groups - 2, groups - 1, False, iteration_steps(True, False, False)))
    parts.append((groups - 1, groups, False, iteration_steps(False, False, False)))
    out, at = [], 0
    for first, end, looped, steps in parts:
        jobs = [s for s in steps if s[0] in "TCW"]
        out.append((first, end, looped, steps, at, len(jobs)))
        at += len(jobs) * (end - first)
    return out


def gnn_kernel(nc, x, adj, w_left, w_right, w_lin, b_lin, ln_a, ln_b, h1, out):
    B, S, _ = adj.shape
    H = x.shape[2]
    L = w_left.shape[0]
    P = 128
    KC = H // P
    HALF = H // 2
    HC = KC // 2
    ROWS = TILES * P
    PER = B * S // ROWS
    GROUPS = L * PER
    M_JOBS = 2 * KC + 2 * TILES
    H_JOB = 2 * KC
    W_JOBS = 3 * KC
    INV_TEMPER = 1.0 / float(H) ** 0.5
    DDOF = H / (H - 1.0)
    EPS_STD, EPS_SUM, EPS_LN = 1e-3, 1e-10, 1e-5
    assert 2 * S == P and H == 2 * HALF and L == 2 and TILES == 4 and KC == 6
    PARTS = regions(GROUPS)
    weights = (w_left, w_right, w_lin)

    x_rows = x.rearrange("b s h -> (b s) h")
    out_rows = out.rearrange("b s h -> (b s) h")
    adj_group = adj.rearrange("(g t b) i j -> g (b i) t j", g=PER, t=TILES)

    with ExitStack() as ctx:
        def sb(name, shape, dt):
            return ctx.enter_context(nc.sbuf_tensor(name, shape, dt))

        def sem(name):
            return ctx.enter_context(nc.semaphore(name))

        wt = sb("wt", [P, 3, 2, KC, H], F32R)
        ht = sb("ht", [P, KC, TILES, 2, P], F32R)
        mt = sb("mt", [P, 2, 2, 2, ROWS], F32R)
        hl = sb("hl", [P, 3, 2, H], F32R)
        rows = sb("rows", [P, 3, H], F32)
        side = sb("side", [P, 4, H], F32)
        vec = sb("vec", [P, 3, H], F32)
        ebd = sb("ebd", [P, TILES, P], F32)
        et = sb("et", [P, TILES, 2, P], F32R)
        mask = sb("mask", [P, TILES, 3, S], F32)
        us = sb("us", [P, TILES, S], F32)
        ident = sb("ident", [P, P], F32)
        upper = sb("upper", [P, S], BF16)
        lower = sb("lower", [P, S], BF16)
        powers = sb("powers", [P, 2], F32)
        stats = sb("stats", [P, 2, 6], F32)
        xstats = sb("xstats", [P, 2, 6], F32)
        mom = sb("mom", [P, TILES, 2], F32)
        xmom = sb("xmom", [P, TILES, 2], F32)
        col = sb("col", [P, 9, TILES], F32)
        ESUM, VAR, STD, FLOOR, DEN, SCALE, XVAR, XRSTD, XSHIFT = range(9)

        parted = [side[:, p, 0:8 * S].rearrange("p (t a m j) -> p t a m j", t=2, a=2, m=2) for p in range(2)]

        pm = ctx.enter_context(nc.psum_tensor("pm", [P, M_BANKS, 512], F32))
        pu = ctx.enter_context(nc.psum_tensor("pu", [P, TILES, 4 * P], F32))
        pc = ctx.enter_context(nc.psum_tensor("pc", [P, C_BANKS, 512], F32))

        const_base = sem("const_base")
        const_ready = sem("const_ready")
        vec_loaded = sem("vec_loaded")
        adj_loaded = sem("adj_loaded")
        x_loaded = [sem(f"x_loaded{i}") for i in range(3)]
        res_loaded = [sem(f"res_loaded{i}") for i in range(2)]
        w_loaded = [sem(f"w_loaded{i}") for i in range(4)]
        stored = [sem(f"stored{i}") for i in range(2)]
        m_full = sem("m_full")
        m_hi = sem("m_hi")
        m_clear = sem("m_clear")
        c_full = sem("c_full")
        ht_hi = sem("ht_hi")
        w_hi = sem("w_hi")
        c_clear = sem("c_clear")
        u_full = sem("u_full")
        u_cross = sem("u_cross")
        u_joined = sem("u_joined")
        u_whole = sem("u_whole")
        u_masked = sem("u_masked")
        u_summed = sem("u_summed")
        e_exp = sem("e_exp")
        e_masked = sem("e_masked")
        et_full = sem("et_full")
        et_hi = sem("et_hi")
        et_clear = sem("et_clear")
        a_full = sem("a_full")
        mask_ready = sem("mask_ready")
        c_stats = sem("c_stats")
        c_moments = sem("c_moments")
        c_var = sem("c_var")
        c_floor = sem("c_floor")
        c_std = sem("c_std")
        c_den = sem("c_den")
        c_scale = sem("c_scale")
        f_centred = sem("f_centred")
        f_affine = sem("f_affine")
        f_done = sem("f_done")
        x_stats = sem("x_stats")
        x_moments = sem("x_moments")
        x_eps = sem("x_eps")
        x_var = sem("x_var")
        x_rstd = sem("x_rstd")
        x_shift = sem("x_shift")
        x_norm = sem("x_norm")

        def ht_half(t, half, part):
            return ht[:, half * HC:(half + 1) * HC, t, part, :].rearrange("p c (n b) -> p c b n", b=2)

        def by_graph(tiles):
            return tiles.rearrange("p c (b n) -> p c b n", b=2)

        def mt_part(k, part):
            return mt[:, k // 2 % 2, part, k % 2, :].rearrange("p (t b n) -> p t b n", t=TILES, b=2)

        def by_node(bank):
            return bank.rearrange("p (t n b) -> p t b n", t=TILES, b=2)

        def ring_after(part, G, step, halves=2):
            first, _, _, steps, at, grow = part
            jobs = [s for s in steps if s[0] in "TCW"]
            return 2 * grow * (G - first) + 2 * (at + jobs.index(step)) + halves

        def tile_count(G, n, per=1):
            return 4 * per * G + per * n

        def pair_count(G, n, per=1):
            return 2 * per * G + per * n

        def x_load_count(G, t):
            return 32 * G + (32 if t == 3 else 16) if t in (0, 3) else 16 * G + 16

        def w_slot(G, step):
            order = [s for p in PARTS for s in p[3] if s[0] == "W"]
            layer = 0 if G < 0 else 1
            i = order.index(step, W_JOBS * layer)
            if layer == 0:
                return i, i % 4, 16 * (i // 4 + 1)
            i1 = i - W_JOBS
            used = len(range(2 + i1 % 2, W_JOBS, 4))
            return i, 2 + i1 % 2, 16 * (used + i1 // 2 + 1)

        def result(part, t):
            return rows[:, t - 2, :] if part[0] == GROUPS - 1 and t >= 2 else side[:, t % 2, :]

        def wait_from(engine, semaphore, value):
            if isinstance(value, int) and value <= 0:
                return
            engine.wait_ge(semaphore, value)

        def each_part(engine, walk):
            for part in PARTS:
                first, end, looped = part[:3]
                if looped:
                    with engine.Fori(first, end) as G:
                        walk(part, G)
                else:
                    walk(part, first)

        def load_weights(engine, i):
            layer = i // W_JOBS
            _, mat, ob = [s for p in PARTS for s in p[3] if s[0] == "W"][i]
            slot = i % 4 if layer == 0 else 2 + i % 2
            engine.dma_start(side[:, slot, :], weights[mat][layer, ob * P:(ob + 1) * P, :]).then_inc(w_loaded[slot], 16)

        block = ctx.enter_context(nc.Block())

        @block.sync
        def _(sp):
            def load_vectors(layer):
                for i, v in enumerate((b_lin, ln_a, ln_b)):
                    sp.dma_start(vec[:, i, :], v[layer:layer + 1, :].to_broadcast([P, H])).then_inc(vec_loaded, 16)

            def load_adjacency(g):
                for copy in (ADJ, MR):
                    sp.dma_start(mask[:, :, copy, :], adj_group[g]).then_inc(adj_loaded, 16)

            def load_rows(source, g, t):
                sp.dma_start(rows[:, H_SLOTS[t], :], source[bass.ds((g * TILES + t) * P, P), :]).then_inc(
                    x_loaded[H_SLOTS[t]], 16)

            def load_residual(row_tile, t):
                sp.dma_start(side[:, 2 + t % 2, :], x_rows[bass.ds(row_tile * P, P), :]).then_inc(res_loaded[t % 2], 16)

            for t in range(3):
                load_rows(x_rows, 0, t)
                if t > 0:
                    load_weights(sp, 2 * t - 2)
                    load_weights(sp, 2 * t - 1)
            load_adjacency(0)
            load_vectors(0)

            def walk(part, G):
                first, end, looped, steps, _, _ = part
                layer = 1 if first >= PER else 0
                g = G - PER * layer
                for step in steps:
                    kind = step[0]
                    if kind == "T":
                        on, t = LOADED_BY[step[1]]
                        g2_first = first + 1 + on
                        if g2_first < GROUPS:
                            sp.wait_ge(c_full, ring_after(part, G, step))
                            if g2_first < PER:
                                load_rows(x_rows, G + 1 + on, t)
                            else:
                                g2 = G + 1 + on - PER
                                if first < PER:
                                    sp.wait_ge(stored[t % 2], 32 * g2 + 16 * (t // 2) + 16)
                                load_rows(h1, g2, t)
                    if kind == "adj":
                        sp.wait_ge(e_masked, tile_count(G, 4, 2))
                        nxt = 0 if first == PER - 1 else g + 1
                        load_adjacency(nxt)
                    if kind == "W" and w_slot(first, step)[0] >= 2 * W_JOBS - 2:
                        sp.wait_ge(c_full, ring_after(part, G, step))
                        load_residual(w_slot(first, step)[0] % 2, w_slot(first, step)[0] % 2)
                    if kind == "F":
                        t = step[1]
                        dest = out_rows if layer else h1
                        sp.wait_ge(f_done, tile_count(G, t + 1))
                        sp.dma_start(dest[bass.ds((g * TILES + t) * P, P), :], result(part, t)).then_inc(stored[t % 2], 16)
                        if layer and (first < GROUPS - 1 or t < 2):
                            load_residual(g * TILES + t + 2, t)
                        if first == PER - 1 and t == 3:
                            load_vectors(1)
                    if first == PER - 2 and step == ("N", 3, 1):
                        for i in range(W_JOBS, W_JOBS + 2):
                            load_weights(sp, i)
                if first == PER - 1:
                    for t in range(2):
                        sp.wait_ge(stored[t], 32 * PER)

            each_part(sp, walk)
            for t in range(2):
                sp.wait_ge(stored[t], 16 * 2 * GROUPS)

        @block.gpsimd
        def _(pool):
            nc.gpsimd.memset(ident[:], 0.0).then_inc(const_base, 1)
            nc.gpsimd.memset(upper[:], 1.0).then_inc(const_base, 1)
            nc.gpsimd.memset(lower[:], 1.0).then_inc(const_base, 1)
            nc.gpsimd.memset(ebd[:], 0.0).then_inc(const_ready, 1)
            nc.gpsimd.memset(powers[:, 0:1], 0.5).then_inc(const_ready, 1)
            nc.gpsimd.memset(powers[:, 1:2], -0.5).then_inc(const_ready, 1)
            pool.wait_ge(const_base, 3)
            pool.wait_ge(const_ready, 3)
            nc.gpsimd.affine_select(out=ident[:], in_=ident[:], compare_op=ALU.not_equal, fill=1.0, base=0,
                                    pattern=[[1, P]], channel_multiplier=-1).then_inc(const_ready, 1)
            for b in range(2):
                own = slice(b * S, (b + 1) * S)
                pool.wait_ge(const_ready, 4 + 2 * b)
                nc.gpsimd.affine_select(out=upper[own, :], in_=upper[own, :], compare_op=ALU.is_ge, fill=0.0, base=0,
                                        pattern=[[1, S]], channel_multiplier=-1).then_inc(const_ready, 1)
                pool.wait_ge(const_ready, 5 + 2 * b)
                nc.gpsimd.affine_select(out=lower[own, :], in_=lower[own, :], compare_op=ALU.is_gt, fill=0.0, base=0,
                                        pattern=[[-1, S]], channel_multiplier=1).then_inc(const_ready, 1)
            pool.wait_ge(const_ready, 8)

            def walk(part, G):
                first, end, looped, steps, _, _ = part
                for step in steps:
                    kind = step[0]
                    if kind == "C":
                        t = step[1]
                        pool.wait_ge(c_var, tile_count(G, t + 1))
                        nc.gpsimd.tensor_tensor(col[:, STD, t:t + 1], col[:, VAR, t:t + 1], powers[:, 0:1],
                                                ALU.pow).then_inc(c_std, 1)
                    if kind == "X":
                        t = step[1]
                        pool.wait_ge(x_var, tile_count(G + step[2], t + 1))
                        nc.gpsimd.tensor_tensor(col[:, XRSTD, t:t + 1], col[:, XVAR, t:t + 1], powers[:, 1:2],
                                                ALU.pow).then_inc(x_rstd, 1)

            each_part(pool, walk)

        @block.tensor
        def _(pe):
            pe.wait_ge(const_ready, 8)

            def transposes(part, G, step, source):
                for half in range(2):
                    pe.wait_ge(c_clear, ring_after(part, G, step, half - 1) + C_BANKS)
                    for j in range(HC):
                        kc = half * HC + j
                        last = nc.tensor.transpose(pc[:, half, j * P:(j + 1) * P], source[:, kc * P:(kc + 1) * P], ident[:])
                    last.then_inc(c_full, 1)

            def project(k, t0, t1, c0, c1):
                oc, lr = k // 2, k % 2
                for kc in range(c0, c1):
                    for n, (a, b) in enumerate(PASSES):
                        last = nc.tensor.matmul(pm[:, k % M_BANKS, t0 * P:t1 * P], wt[:, lr, a, kc, oc * P:(oc + 1) * P],
                                                ht[:, kc, t0:t1, b, :], start=(kc == 0 and n == 0),
                                                stop=(kc == KC - 1 and n == len(PASSES) - 1))
                return last

            def walk(part, G):
                first, end, looped, steps, _, _ = part
                N = G + 1
                fresh = first in (-1, PER - 1)
                for step in steps:
                    kind = step[0]
                    if kind == "T":
                        t = step[1]
                        if first + 1 < PER:
                            pe.wait_ge(x_norm, tile_count(N, t + 1))
                        else:
                            pe.wait_ge(x_loaded[H_SLOTS[t]], x_load_count(N, t))
                        transposes(part, G, step, rows[:, H_SLOTS[t], :])
                    elif kind == "W":
                        _, slot, count = w_slot(first, step)
                        pe.wait_ge(w_loaded[slot], count)
                        transposes(part, G, step, side[:, slot, :])
                    elif kind == "M":
                        k, t0, t1, c0, c1 = step[1:]
                        if t0 == 0 and c0 == 0:
                            pe.wait_ge(m_clear, M_JOBS * N + k - M_BANKS + 1 + M_BANKS)
                            if fresh:
                                pe.wait_ge(c_clear, ring_after(part, G, ("W", k % 2, k // 2)) + C_BANKS)
                        if k < 2:
                            pe.wait_ge(c_clear, ring_after(part, G, ("T", t1 - 1)) + C_BANKS)
                        last = project(*step[1:])
                        if t1 == TILES and c1 == KC:
                            last.then_inc(m_full, 1)
                    elif kind == "S":
                        oc = step[1]
                        Q = G if oc == KC - 1 else N
                        pe.wait_ge(m_clear, M_JOBS * Q + 2 * oc + 2 + M_BANKS)
                        if oc == 0:
                            pe.wait_ge(mask_ready, 3 * N + 3)
                        for t in range(TILES):
                            for b in range(2):
                                own = slice(t * P + b * S, t * P + (b + 1) * S)
                                h_parts = ht[:, oc, t].rearrange("p a (n b) -> p b (a n)", b=2)
                                last = nc.tensor.matmul(
                                    pu[:, t, b * 2 * P:(b + 1) * 2 * P], h_parts[:, b, :], mt[:, oc % 2, :, :, own],
                                    start=(oc == 0 and b == 0), stop=(oc == KC - 1), skip_group_check=True)
                            if oc == KC - 1:
                                last.then_inc(u_full, 1)
                    elif kind == "H":
                        t, half = step[1:]
                        j = H_JOB + 2 * t + half
                        pe.wait_ge(m_clear, M_JOBS * G + j - M_BANKS + 1 + M_BANKS)
                        n = 0
                        for kc in range(KC):
                            for a, b in PASSES:
                                last = nc.tensor.matmul(
                                    pm[:, j % M_BANKS, 0:HALF], ht[:, kc, t, a, :],
                                    wt[:, LIN, b, kc, half * HALF:(half + 1) * HALF],
                                    start=(n == 0), stop=(n == 3 * KC - 1))
                                n += 1
                        last.then_inc(m_full, 1)
                    elif kind == "ET":
                        p = step[1]
                        pe.wait_ge(e_masked, pair_count(G, p + 1, 4))
                        for t in range(2 * p, 2 * p + 2):
                            last = nc.tensor.transpose(pu[:, t, 0:P], ebd[:, t, :], ident[:])
                        last.then_inc(et_full, 1)
                    elif kind == "A":
                        pe.wait_ge(adj_loaded, 32 * N + 32)
                        wait_from(pe, et_clear, pair_count(N, 0))
                        for t in range(TILES):
                            last = nc.tensor.transpose(pu[:, t, 0:P], mask[:, t, ADJ:MR + 1, :].rearrange("p a b -> p (a b)"), ident[:])
                        last.then_inc(a_full, 1)
                    elif kind == "C":
                        t = step[1]
                        pe.wait_ge(et_clear, pair_count(G, t // 2 + 1))
                        pe.wait_ge(m_clear, M_JOBS * G + H_JOB + 2 * t + 2 + M_BANKS)
                        for half in range(2):
                            pe.wait_ge(c_clear, ring_after(part, G, step, half - 1) + C_BANKS)
                            for n, (a, b) in enumerate(PASSES):
                                last = nc.tensor.matmul(
                                    pc[:, half, 0:HALF], et[:, t, a, :],
                                    hl[:, H_SLOTS[t], b, half * HALF:(half + 1) * HALF], start=(n == 0), stop=(n == 2))
                            last.then_inc(c_full, 1)
                if fresh:
                    pe.wait_ge(c_clear, ring_after(part, G, [s for s in steps if s[0] == "W"][-1]) + C_BANKS)

            each_part(pe, walk)

        @block.scalar
        def _(act):
            def walk(part, G):
                first, end, looped, steps, _, _ = part
                N = G + 1
                layer = 1 if first >= PER else 0
                for step in steps:
                    kind = step[0]
                    if kind in ("T", "W"):
                        for half in range(2):
                            act.wait_ge(c_full, ring_after(part, G, step, half + 1))
                            src = pc[:, half, 0:HALF].rearrange("p (c n) -> p c n", c=HC)
                            if kind == "T":
                                nc.scalar.copy(ht_half(step[1], half, HI), by_graph(src)).then_inc(ht_hi, 1)
                            else:
                                mat, ob = step[1:]
                                dst = wt[:, mat, HI, half * HC:(half + 1) * HC, ob * P:(ob + 1) * P]
                                nc.scalar.copy(dst, src).then_inc(w_hi, 1)
                        if kind == "W":
                            i = w_slot(first, step)[0]
                            on = 4 if i < W_JOBS else 2
                            if i % W_JOBS + on < W_JOBS:
                                load_weights(act, i + on)
                    elif kind == "M" and step[3] == TILES and step[5] == KC:
                        k = step[1]
                        act.wait_ge(m_full, M_JOBS * N + k + 1)
                        nc.scalar.copy(mt_part(k, HI), by_node(pm[:, k % M_BANKS, :])).then_inc(m_hi, 1)
                    elif kind == "H":
                        t, half = step[1:]
                        j = H_JOB + 2 * t + half
                        act.wait_ge(m_full, M_JOBS * G + j + 1)
                        nc.scalar.copy(hl[:, H_SLOTS[t], HI, half * HALF:(half + 1) * HALF],
                                       pm[:, j % M_BANKS, 0:HALF]).then_inc(m_hi, 1)
                    elif kind == "U":
                        p = step[1]
                        wait_from(act, stored[p], 32 * G)
                        act.wait_ge(u_full, tile_count(G, 2 * p + 2))
                        for b in range(2):
                            near, far = slice(b * S, (b + 1) * S), slice((1 - b) * S, (2 - b) * S)
                            nc.scalar.copy(parted[p][near].rearrange("p t a m j -> p t (a m j)"),
                                           pu[far, 2 * p:2 * p + 2, b * 2 * P:(b + 1) * 2 * P]).then_inc(u_cross, 1)
                    elif kind == "EX":
                        p = step[1]
                        pair = us[:, 2 * p:2 * p + 2, :]
                        act.wait_ge(u_summed, pair_count(G, p + 1))
                        nc.scalar.activation(pair, pair, ACT.Exp, scale=INV_TEMPER).then_inc(e_exp, 1)
                    elif kind == "ET":
                        p = step[1]
                        pair = slice(2 * p, 2 * p + 2)
                        act.wait_ge(et_full, pair_count(G, p + 1))
                        nc.scalar.copy(et[:, pair, HI, :], pu[:, pair, 0:P]).then_inc(et_hi, 1)
                    elif kind == "N":
                        t = step[1]
                        act.wait_ge(x_shift, tile_count(G + step[2], t + 1))
                        row = rows[:, H_SLOTS[t], :]
                        nc.scalar.activation(row, row, ACT.Relu, bias=col[:, XSHIFT, t:t + 1],
                                             scale=col[:, XRSTD, t:t + 1]).then_inc(x_norm, 1)
                    elif kind == "F" and layer == 0:
                        t = step[1]
                        act.wait_ge(f_affine, tile_count(G, t + 1))
                        nc.scalar.activation(side[:, t % 2, :], side[:, t % 2, :], ACT.Relu).then_inc(f_done, 1)

            each_part(act, walk)

        @block.vector
        def _(dve):
            nc.vector.memset(us[:, 0, 0:1], 0.0).then_inc(m_clear, M_BANKS)
            nc.vector.memset(us[:, 0, 1:2], 0.0).then_inc(c_clear, C_BANKS)
            dve.wait_ge(const_ready, 8)

            def low_part(dst, src, hi):
                return nc.vector.tensor_tensor(dst, src, hi.bitcast(F32), ALU.subtract)

            def walk(part, G):
                first, end, looped, steps, _, _ = part
                N = G + 1
                layer = 1 if first >= PER else 0
                for step in steps:
                    kind = step[0]
                    if kind in ("T", "W"):
                        for half in range(2):
                            src = pc[:, half, 0:HALF].rearrange("p (c n) -> p c n", c=HC)
                            if kind == "T":
                                t = step[1]
                                dve.wait_ge(ht_hi, tile_count(N, t, 2) + half + 1)
                                op = low_part(ht_half(t, half, LO), by_graph(src), ht_half(t, half, HI))
                            else:
                                mat, ob = step[1:]
                                dve.wait_ge(w_hi, 2 * w_slot(first, step)[0] + half + 1)
                                at = (slice(half * HC, (half + 1) * HC), slice(ob * P, (ob + 1) * P))
                                op = low_part(wt[:, mat, LO, at[0], at[1]], src, wt[:, mat, HI, at[0], at[1]])
                            op.then_inc(c_clear, 1)
                    elif kind == "M" and step[3] == TILES and step[5] == KC:
                        k = step[1]
                        dve.wait_ge(m_hi, M_JOBS * N + k + 1)
                        low_part(mt_part(k, LO), by_node(pm[:, k % M_BANKS, :]), mt_part(k, HI)).then_inc(m_clear, 1)
                    elif kind == "H":
                        t, half = step[1:]
                        j = H_JOB + 2 * t + half
                        dve.wait_ge(m_hi, M_JOBS * G + j + 1)
                        at = slice(half * HALF, (half + 1) * HALF)
                        low_part(hl[:, H_SLOTS[t], LO, at], pm[:, j % M_BANKS, 0:HALF],
                                 hl[:, H_SLOTS[t], HI, at]).then_inc(m_clear, 1)
                    elif kind == "A":
                        dve.wait_ge(a_full, N + 1)
                        nc.vector.tensor_tensor(mask[:, :, ML, :], mask[:, :, ADJ, :],
                                                upper[:].unsqueeze(1).to_broadcast([P, TILES, S]),
                                                ALU.mult).then_inc(mask_ready, 1)
                        for b in range(2):
                            own = slice(b * S, (b + 1) * S)
                            nc.vector.tensor_tensor(mask[own, :, MR, :], pu[own, :, own],
                                                    lower[own, :].unsqueeze(1).to_broadcast([S, TILES, S]),
                                                    ALU.mult).then_inc(mask_ready, 1)
                    elif kind == "U":
                        p = step[1]
                        pair = slice(2 * p, 2 * p + 2)
                        if p == 0:
                            dve.wait_ge(mask_ready, 3 * G + 3)
                        dve.wait_ge(u_cross, pair_count(G, p + 1, 2))
                        for b in range(2):
                            near = slice(b * S, (b + 1) * S)
                            both = parted[p][near].rearrange("p t a m j -> p t (a m j)")
                            nc.vector.tensor_tensor(both, pu[near, pair, b * 2 * P:(b + 1) * 2 * P], both,
                                                    ALU.add).then_inc(u_joined, 1)
                        whole = parted[p][:, :, HI]
                        dve.wait_ge(u_joined, pair_count(G, p + 1, 2))
                        nc.vector.tensor_tensor(whole, whole, parted[p][:, :, LO], ALU.add).then_inc(u_whole, 1)
                        dve.wait_ge(u_whole, pair_count(G, p + 1))
                        nc.vector.tensor_tensor(whole, whole, mask[:, pair, ML:MR + 1:2, :],
                                                ALU.mult).then_inc(u_masked, 1)
                        dve.wait_ge(u_masked, pair_count(G, p + 1))
                        nc.vector.tensor_tensor(us[:, pair, :], whole[:, :, LEFT, :], whole[:, :, RIGHT, :],
                                                ALU.add).then_inc(u_summed, 1)
                    elif kind == "EM":
                        p = step[1]
                        dve.wait_ge(e_exp, pair_count(G, p + 1))
                        for t in range(2 * p, 2 * p + 2):
                            for b in range(2):
                                own = slice(b * S, (b + 1) * S)
                                nc.vector.tensor_tensor_reduce(
                                    out=ebd[own, t, b::2], in0=us[own, t, :], in1=mask[own, t, ADJ, :], scale=1.0,
                                    scalar=0.0, op0=ALU.mult, op1=ALU.add,
                                    accum_out=col[own, ESUM, t:t + 1]).then_inc(e_masked, 1)
                    elif kind == "ET":
                        p = step[1]
                        pair = slice(2 * p, 2 * p + 2)
                        dve.wait_ge(et_hi, pair_count(G, p + 1))
                        low_part(et[:, pair, LO, :], pu[:, pair, 0:P], et[:, pair, HI, :]).then_inc(et_clear, 1)
                    elif kind == "C":
                        t = step[1]
                        if t == 0:
                            dve.wait_ge(vec_loaded, 48 * (layer + 1))
                        if t >= 2 and first < GROUPS - 1:
                            dve.wait_ge(stored[t % 2], 32 * G + 16)
                        context = result(part, t)
                        dve.wait_ge(e_masked, tile_count(G, TILES, 2))
                        for half in range(2):
                            at = slice(half * HALF, (half + 1) * HALF)
                            dve.wait_ge(c_full, ring_after(part, G, step, half + 1))
                            nc.vector.scalar_tensor_tensor(
                                out=context[:, at], in0=vec[:, 0, at], scalar=col[:, ESUM, t:t + 1],
                                in1=pc[:, half, 0:HALF], op0=ALU.mult, op1=ALU.add).then_inc(c_clear, 1)
                        wait_from(dve, c_moments, tile_count(G, t))
                        for half in range(2):
                            dve.wait_ge(c_clear, ring_after(part, G, step, half + 1) + C_BANKS)
                            nc.vector.bn_stats(stats[:, half, :], context[:, half * HALF:(half + 1) * HALF]
                                               ).then_inc(c_stats, 1)
                        dve.wait_ge(c_stats, tile_count(G, t + 1, 2))
                        nc.vector.tensor_scalar(col[:, FLOOR, t:t + 1], col[:, ESUM, t:t + 1], EPS_SUM, EPS_STD,
                                                ALU.add, ALU.mult).then_inc(c_floor, 1)
                        nc.vector.bn_aggr(mom[:, t, :], stats[:].rearrange("p a b -> p (a b)")).then_inc(c_moments, 1)
                        dve.wait_ge(c_moments, tile_count(G, t + 1))
                        nc.vector.tensor_scalar(col[:, VAR, t:t + 1], mom[:, t, 1:2], DDOF, None,
                                                ALU.mult).then_inc(c_var, 1)
                    elif kind == "F":
                        t = step[1]
                        n = tile_count(G, t + 1)
                        row = result(part, t)
                        nc.vector.scalar_tensor_tensor(out=row, in0=row, scalar=mom[:, t, 0:1], in1=vec[:, 1, :],
                                                       op0=ALU.subtract, op1=ALU.mult).then_inc(f_centred, 1)
                        dve.wait_ge(c_std, n)
                        dve.wait_ge(c_floor, n)
                        nc.vector.tensor_tensor(col[:, DEN, t:t + 1], col[:, STD, t:t + 1], col[:, FLOOR, t:t + 1],
                                                ALU.add).then_inc(c_den, 1)
                        dve.wait_ge(c_den, n)
                        nc.vector.reciprocal(col[:, SCALE, t:t + 1], col[:, DEN, t:t + 1]).then_inc(c_scale, 1)
                        dve.wait_ge(c_scale, n)
                        dve.wait_ge(f_centred, n)
                        nc.vector.scalar_tensor_tensor(out=row, in0=row, scalar=col[:, SCALE, t:t + 1],
                                                       in1=vec[:, 2, :], op0=ALU.mult, op1=ALU.add).then_inc(f_affine, 1)
                        if layer:
                            dve.wait_ge(f_affine, n)
                            dve.wait_ge(res_loaded[t % 2], 32 * (G - PER) + 16 * (t // 2) + 16)
                            nc.vector.scalar_tensor_tensor(out=row, in0=row, scalar=0.0, in1=side[:, 2 + t % 2, :],
                                                           op0=ALU.max, op1=ALU.add).then_inc(f_done, 1)
                    elif kind == "X":
                        t = step[1]
                        X = G + step[2]
                        dve.wait_ge(x_loaded[H_SLOTS[t]], x_load_count(X, t))
                        wait_from(dve, x_moments, tile_count(X, t))
                        for half in range(2):
                            nc.vector.bn_stats(xstats[:, half, :],
                                               rows[:, H_SLOTS[t], half * HALF:(half + 1) * HALF]).then_inc(x_stats, 1)
                        dve.wait_ge(x_stats, tile_count(X, t + 1, 2))
                        nc.vector.memset(col[:, XVAR, t:t + 1], EPS_LN).then_inc(x_eps, 1)
                        nc.vector.bn_aggr(xmom[:, t, :], xstats[:].rearrange("p a b -> p (a b)")).then_inc(x_moments, 1)
                        dve.wait_ge(x_moments, tile_count(X, t + 1))
                        dve.wait_ge(x_eps, tile_count(X, t + 1))
                        nc.vector.tensor_tensor(col[:, XVAR, t:t + 1], xmom[:, t, 1:2], col[:, XVAR, t:t + 1],
                                                ALU.add).then_inc(x_var, 1)
                    elif kind == "N":
                        t = step[1]
                        X = G + step[2]
                        dve.wait_ge(x_rstd, tile_count(X, t + 1))
                        nc.vector.scalar_tensor_tensor(out=col[:, XSHIFT, t:t + 1], in0=xmom[:, t, 0:1], scalar=-1.0,
                                                       in1=col[:, XRSTD, t:t + 1], op0=ALU.mult,
                                                       op1=ALU.mult).then_inc(x_shift, 1)

            each_part(dve, walk)


_INS = ["x", "adj", "L0_gnn_W_left", "L0_gnn_W_right", "L0_gnn_W_lin", "L0_gnn_b_lin", "L0_gnn_ln_a", "L0_gnn_ln_b"]


def kernel(**inputs):
    import numpy as _np
    import concourse.bacc as _bacc
    from concourse import mybir as _mybir
    from concourse.bass_utils import run_bass_kernel_spmd as _run

    nc = _bacc.Bacc("TRN2", target_bir_lowering=False, num_devices=1)
    arrays, args = {}, []
    for name in _INS:
        a = _np.ascontiguousarray(inputs[name])
        arrays[f"in_{name}_dram"] = a
        args.append(nc.dram_tensor(f"in_{name}_dram", a.shape, _mybir.dt.from_np(a.dtype), kind="ExternalInput").ap())
    shape = inputs["x"].shape
    h1 = nc.dram_tensor("h1_dram", (shape[0] * shape[1], shape[2]), _mybir.dt.float32, kind="Internal").ap()
    out = nc.dram_tensor("out_0_dram", shape, _mybir.dt.float32, kind="ExternalOutput").ap()
    gnn_kernel(nc, *args, h1, out)
    r = _run(nc, [arrays], core_ids=[0])
    return r.results[0]["out_0_dram"]
```

```python
from contextlib import ExitStack

import concourse.bass as bass
from concourse import mybir

F32 = mybir.dt.float32
F32R = mybir.dt.float32r
BF16 = mybir.dt.bfloat16
ALU = mybir.AluOpType
ACT = mybir.ActivationFunctionType

HI, LO = 0, 1
LEFT, RIGHT, LIN = 0, 1, 2
ML, ADJ, MR = 0, 1, 2
PASSES = ((HI, HI), (LO, HI), (HI, LO))

M_BANKS = 2
C_BANKS = 2
TILES = 4
K_SIDES = 12
H_SLOTS = (0, 1, 2, 0)
LOADED_BY = {0: (0, 3), 1: (1, 1), 2: (1, 2), 3: (1, 0)}


def m_parts():
    rows_first = [(k, part) for part in range(2) for k in range(2)]
    return rows_first + [(k, part) for k in range(2, K_SIDES) for part in range(2)]


def m_phase_steps(extra, prepare=()):
    steps = []
    for k, part in m_parts():
        if k < 2:
            amid = extra.get((k, part, "amid"), [])
            for c0, c1 in ((0, 3), (3, 6)) if amid else ((0, 6),):
                steps += [("M", k, 2 * part, 2 * part + 2, c0, c1)] + (amid if c0 == 0 else [])
        elif (k, 0) in extra:
            steps += [("M", k, 0, 4, 3 * part, 3 * part + 3)]
        elif part == 1:
            steps += [("M", k, 0, 4, 0, 6)]
        steps += extra.get((k, part), [])
        oc = k // 2
        if k % 2 == 1 and part == 1 and oc > 0:
            steps += [("S", oc - 1)]
            if oc == 3:
                steps += [("X", t, 2) for t in prepare]
            if oc == 4:
                steps += [("N", t, 2) for t in prepare]
    return steps


def with_weights(extra, placed):
    out = dict(extra)
    for key, step in placed:
        out[key] = [step] + out.get(key, [])
    return out


def iteration_steps(has_next, norm_next, norm_after, weights_h=(), weights_m=()):
    v = [[step] for step in weights_h] + [[]] * 6
    if not has_next:
        return [("H", 0, 0), ("H", 0, 1), ("S", 5), ("U", 0), ("U", 1), ("H", 1, 0), ("EX",), ("EM",), ("EP",),
                ("H", 1, 1), ("H", 2, 0), ("ET",), ("C", 0), ("C", 1), ("H", 2, 1), ("F", 0), ("H", 3, 0), ("C", 2),
                ("H", 3, 1), ("F", 1), ("C", 3), ("F", 2), ("F", 3)]
    steps = [("H", 0, 0), *v[0], ("H", 0, 1), ("S", 5), ("U", 0), ("U", 1), ("H", 1, 0), ("EX",), ("EM",), ("EP",),
             ("T", 0), ("H", 1, 1), ("adj",), *v[1], ("H", 2, 0), ("T", 1), *v[2], ("ET",),
             *[("X", 3, 1)] * norm_next, ("H", 2, 1), ("C", 0), *v[3]]
    steps += [("H", 3, 0), ("T", 2)] + ([("N", 3, 1)] if norm_next else []) + [*v[4], ("H", 3, 1), *v[5], ("T", 3)]
    extra = {(0, 1): [("C", 1)], (1, 1): [("A",), ("F", 0)], (3, 1): [("C", 2)], (4, 1): [("F", 1)],
             (6, 1): [("C", 3)], (7, 1): [("F", 2)], (8, 1): [("F", 3)]}
    return steps + m_phase_steps(with_weights(extra, weights_m), (0, 1, 2) if norm_after else ())


def regions(groups):
    sides = [("V", m, b) for b in range(6) for m in (LEFT, RIGHT)]
    lins = [("W", LIN, b) for b in range(6)]
    start = [("X", 0, 1), ("N", 0, 1), ("X", 1, 1), ("N", 1, 1), ("X", 2, 1), ("T", 0), sides[0], ("T", 1),
             ("N", 2, 1), sides[1], ("X", 3, 1)]
    placed = [((k - 2, 1), sides[k]) for k in range(2, 12)] + [((k, 0), lins[k - 5]) for k in range(5, 11)]
    extra = {(0, 0): [("T", 2), ("N", 3, 1)], (1, 0, "amid"): [("T", 3)], (1, 1): [("A",)]}
    parts = [(-1, 0, False, start + m_phase_steps(with_weights(extra, placed), (0, 1, 2)))]
    half = groups // 2
    steady0 = iteration_steps(True, True, True)
    parts.append((0, 1, False, steady0))
    parts.append((1, half - 2, True, steady0))
    parts.append((half - 2, half - 1, False, iteration_steps(True, True, False)))
    mixed = [sides[6], sides[7], lins[0], sides[8], lins[1], sides[9], lins[2], sides[10], lins[3], sides[11],
             *lins[4:]]
    placed = [((k, 0), mixed[k]) for k in range(12)]
    parts.append((half - 1, half, False, iteration_steps(True, False, False, sides[:6], placed)))
    parts.append((half, groups - 2, True, iteration_steps(True, False, False)))
    parts.append((groups - 2, groups - 1, False, iteration_steps(True, False, False)))
    parts.append((groups - 1, groups, False, iteration_steps(False, False, False)))
    out, at = [], 0
    for first, end, looped, steps in parts:
        jobs = [s for s in steps if s[0] in "TCW"]
        out.append((first, end, looped, steps, at, len(jobs)))
        at += len(jobs) * (end - first)
    return out


def gnn_kernel(nc, x, adj, w_left, w_right, w_lin, b_lin, ln_a, ln_b, h1, adj_t, out):
    B, S, _ = adj.shape
    H = x.shape[2]
    L = w_left.shape[0]
    P = 128
    KC = H // P
    HALF = H // 2
    HC = KC // 2
    ROWS = TILES * P
    PER = B * S // ROWS
    GROUPS = L * PER
    M_JOBS = 2 * KC + 2 * TILES
    H_JOB = 2 * KC
    W_JOBS = 3 * KC
    SUMS = 2
    INV_TEMPER = 1.0 / float(H) ** 0.5
    DDOF = H / (H - 1.0)
    EPS_STD, EPS_SUM, EPS_LN = 1e-3, 1e-10, 1e-5
    assert 2 * S == P and H == 2 * HALF and L == 2 and TILES == 4 and KC == 6
    PARTS = regions(GROUPS)
    WEIGHT_STEPS = [s for p in PARTS for s in p[3] if s[0] in "VW"]
    weights = (w_left, w_right, w_lin)

    x_rows = x.rearrange("b s h -> (b s) h")
    out_rows = out.rearrange("b s h -> (b s) h")
    adj_group = adj.rearrange("(g t b) i j -> g (b i) t j", g=PER, t=TILES)

    with ExitStack() as ctx:
        def sb(name, shape, dt):
            return ctx.enter_context(nc.sbuf_tensor(name, shape, dt))

        def sem(name):
            return ctx.enter_context(nc.semaphore(name))

        wt = sb("wt", [P, 3, 2, KC, H], F32R)
        ht = sb("ht", [P, KC, TILES, 2, P], F32R)
        gt = sb("gt", [P, 2, 2, 2, ROWS], F32R)
        hl = sb("hl", [P, 3, 2, SUMS + H], F32R)
        rows = sb("rows", [P, 3, H], F32)
        side = sb("side", [P, 4, H], F32)
        vec = sb("vec", [P, 3, H], F32)
        ebd = sb("ebd", [P, TILES, P], F32)
        et = sb("et", [P, TILES, 2, P], F32R)
        mask = sb("mask", [P, TILES, 3, S], F32)
        us = sb("us", [P, TILES, S], F32)
        ident = sb("ident", [P, P], F32)
        until = sb("until", [P, S], BF16)
        beyond = sb("beyond", [P, S], BF16)
        unit = sb("unit", [P, 2, SUMS], F32)
        powers = sb("powers", [P, 2], F32)
        stats = sb("stats", [P, 2, 6], F32)
        xstats = sb("xstats", [P, 2, 6], F32)
        mom = sb("mom", [P, TILES, 2], F32)
        xmom = sb("xmom", [P, TILES, 2], F32)
        col = sb("col", [P, 9, TILES], F32)
        ESUM, VAR, STD, FLOOR, DEN, SCALE, XVAR, XRSTD, XSHIFT = range(9)

        parted = [side[:, p, 0:8 * S].rearrange("p (t a m j) -> p t a m j", t=2, a=2, m=2) for p in range(2)]

        pm = ctx.enter_context(nc.psum_tensor("pm", [P, M_BANKS, 512], F32))
        pu = ctx.enter_context(nc.psum_tensor("pu", [P, TILES, 4 * P], F32))
        pc = ctx.enter_context(nc.psum_tensor("pc", [P, C_BANKS, 512], F32))

        const_base = sem("const_base")
        const_ready = sem("const_ready")
        vec_loaded = sem("vec_loaded")
        adj_loaded = sem("adj_loaded")
        adj_t_stored = sem("adj_t_stored")
        x_loaded = [sem(f"x_loaded{i}") for i in range(3)]
        res_loaded = [sem(f"res_loaded{i}") for i in range(2)]
        w_loaded = [sem(f"w_loaded{i}") for i in range(4)]
        stored = [sem(f"stored{i}") for i in range(2)]
        m_full = sem("m_full")
        m_hi = sem("m_hi")
        m_clear = sem("m_clear")
        c_full = sem("c_full")
        ht_hi = sem("ht_hi")
        w_hi = sem("w_hi")
        v_hi = sem("v_hi")
        v_split = sem("v_split")
        unit_ready = sem("unit_ready")
        c_clear = sem("c_clear")
        u_full = sem("u_full")
        u_cross = sem("u_cross")
        u_joined = sem("u_joined")
        u_whole = sem("u_whole")
        u_masked = sem("u_masked")
        u_summed = sem("u_summed")
        e_exp = sem("e_exp")
        e_masked = sem("e_masked")
        e_moved = sem("e_moved")
        et_hi = sem("et_hi")
        et_split = sem("et_split")
        a_full = sem("a_full")
        mask_ready = sem("mask_ready")
        c_sum = sem("c_sum")
        c_stats = sem("c_stats")
        c_moments = sem("c_moments")
        c_var = sem("c_var")
        c_floor = sem("c_floor")
        c_std = sem("c_std")
        c_den = sem("c_den")
        c_scale = sem("c_scale")
        f_centred = sem("f_centred")
        f_affine = sem("f_affine")
        f_done = sem("f_done")
        x_stats = sem("x_stats")
        x_moments = sem("x_moments")
        x_eps = sem("x_eps")
        x_var = sem("x_var")
        x_rstd = sem("x_rstd")
        x_shift = sem("x_shift")
        x_norm = sem("x_norm")

        def ht_half(t, half, part):
            return ht[:, half * HC:(half + 1) * HC, t, part, :].rearrange("p c (n b) -> p c b n", b=2)

        def by_graph(tiles):
            return tiles.rearrange("p c (b n) -> p c b n", b=2)

        def gt_part(k, part):
            return gt[:, k // 2 % 2, part, k % 2, :].rearrange("p (t b n) -> p t b n", t=TILES, b=2)

        def by_node(bank):
            return bank.rearrange("p (t n b) -> p t b n", t=TILES, b=2)

        def ring_after(part, G, step, halves=2):
            first, _, _, steps, at, grow = part
            jobs = [s for s in steps if s[0] in "TCW"]
            return 2 * grow * (G - first) + 2 * (at + jobs.index(step)) + halves

        def tile_count(G, n, per=1):
            return 4 * per * G + per * n

        def pair_count(G, n, per=1):
            return 2 * per * G + per * n

        def mask_count(layer, N):
            return 2 * (N - PER) + 5 * PER + 2 if layer else 5 * N + 5

        def x_load_count(G, t):
            return 32 * G + (32 if t == 3 else 16) if t in (0, 3) else 16 * G + 16

        def w_slot(G, step):
            layer = 0 if G < 0 else 1
            i = WEIGHT_STEPS.index(step, W_JOBS * layer)
            if layer == 0:
                return i, i % 4, 16 * (i // 4 + 1)
            i1 = i - W_JOBS
            used = len(range(2 + i1 % 2, W_JOBS, 4))
            return i, 2 + i1 % 2, 16 * (used + i1 // 2 + 1)

        def kind_count(G, step):
            return sum(s[0] == step[0] for s in WEIGHT_STEPS[:w_slot(G, step)[0] + 1])

        def wait_block_read(engine, part, G, step):
            if step[0] == "V":
                engine.wait_ge(v_split, kind_count(part[0], step))
            else:
                engine.wait_ge(c_full, ring_after(part, G, step))

        def next_block(G, step):
            i = w_slot(G, step)[0]
            on = 4 if i < W_JOBS else 2
            return i + on if i % W_JOBS + on < W_JOBS else None

        def result(part, t):
            return rows[:, t - 2, :] if part[0] == GROUPS - 1 and t >= 2 else side[:, t % 2, :]

        def wait_from(engine, semaphore, value):
            if isinstance(value, int) and value <= 0:
                return
            engine.wait_ge(semaphore, value)

        def each_part(engine, walk):
            for part in PARTS:
                first, end, looped = part[:3]
                if looped:
                    with engine.Fori(first, end) as G:
                        walk(part, G)
                else:
                    walk(part, first)

        def load_weights(engine, i):
            layer = i // W_JOBS
            kind, mat, ob = WEIGHT_STEPS[i]
            slot = i % 4 if layer == 0 else 2 + i % 2
            own = slice(ob * P, (ob + 1) * P)
            if kind == "W":
                engine.dma_start(side[:, slot, :], weights[mat][layer, own, :]).then_inc(w_loaded[slot], 16)
            else:
                engine.dma_start(side[:, slot, :].rearrange("p (c n) -> p c n", c=KC),
                                 weights[mat][layer, :, own].rearrange("(c p) n -> p c n", p=P)
                                 ).then_inc(w_loaded[slot], 16)

        block = ctx.enter_context(nc.Block())

        @block.sync
        def _(sp):
            def load_vectors(layer):
                for i, v in enumerate((b_lin, ln_a, ln_b)):
                    sp.dma_start(vec[:, i, :], v[layer:layer + 1, :].to_broadcast([P, H])).then_inc(vec_loaded, 16)

            def load_adjacency(layer, g):
                sp.dma_start(mask[:, :, ADJ, :], adj_t[g] if layer else adj_group[g]).then_inc(adj_loaded, 16)
                sp.dma_start(mask[:, :, MR, :], adj_group[g]).then_inc(adj_loaded, 16)

            def load_rows(source, g, t):
                sp.dma_start(rows[:, H_SLOTS[t], :], source[bass.ds((g * TILES + t) * P, P), :]).then_inc(
                    x_loaded[H_SLOTS[t]], 16)

            def load_residual(row_tile, t):
                sp.dma_start(side[:, 2 + t % 2, :], x_rows[bass.ds(row_tile * P, P), :]).then_inc(res_loaded[t % 2], 16)

            for t in range(3):
                load_rows(x_rows, 0, t)
                if t > 0:
                    load_weights(sp, 2 * t - 2)
                    load_weights(sp, 2 * t - 1)
            load_adjacency(0, 0)
            load_vectors(0)

            def walk(part, G):
                first, end, looped, steps, _, _ = part
                layer = 1 if first >= PER else 0
                g = G - PER * layer
                for step in steps:
                    kind = step[0]
                    if kind == "T":
                        on, t = LOADED_BY[step[1]]
                        g2_first = first + 1 + on
                        if g2_first < GROUPS:
                            sp.wait_ge(c_full, ring_after(part, G, step))
                            if g2_first < PER:
                                load_rows(x_rows, G + 1 + on, t)
                            else:
                                g2 = G + 1 + on - PER
                                if first < PER:
                                    sp.wait_ge(stored[t % 2], 32 * g2 + 16 * (t // 2) + 16)
                                load_rows(h1, g2, t)
                    if kind == "adj":
                        sp.wait_ge(e_masked, G + 1)
                        if not layer:
                            sp.wait_ge(adj_t_stored, 16 * G + 16)
                        if first == PER - 1:
                            load_adjacency(1, 0)
                        else:
                            load_adjacency(layer, g + 1)
                    if kind == "A" and first + 1 < PER:
                        sp.wait_ge(mask_ready, mask_count(0, G + 1))
                        sp.dma_start(adj_t[G + 1], mask[:, :, ADJ, :]).then_inc(adj_t_stored, 16)
                    if kind == "EP":
                        sp.wait_ge(e_masked, G + 1)
                        for b in range(2):
                            own = slice(b * S, (b + 1) * S)
                            sp.dma_start(ebd[b::2, :, own], us[own, :, :]).then_inc(e_moved, 16)
                    if kind == "V" and next_block(first, step):
                        wait_block_read(sp, part, G, step)
                        load_weights(sp, next_block(first, step))
                    if kind in "VW" and w_slot(first, step)[0] >= 2 * W_JOBS - 2:
                        wait_block_read(sp, part, G, step)
                        load_residual(w_slot(first, step)[0] % 2, w_slot(first, step)[0] % 2)
                    if kind == "F":
                        t = step[1]
                        dest = out_rows if layer else h1
                        sp.wait_ge(f_done, tile_count(G, t + 1))
                        sp.dma_start(dest[bass.ds((g * TILES + t) * P, P), :], result(part, t)).then_inc(
                            stored[t % 2], 16)
                        if layer and (first < GROUPS - 1 or t < 2):
                            load_residual(g * TILES + t + 2, t)
                        if first == PER - 1 and t == 3:
                            load_vectors(1)
                    if first == PER - 2 and step == ("N", 3, 1):
                        for i in range(W_JOBS, W_JOBS + 2):
                            load_weights(sp, i)
                if first == PER - 1:
                    for t in range(2):
                        sp.wait_ge(stored[t], 32 * PER)

            each_part(sp, walk)
            for t in range(2):
                sp.wait_ge(stored[t], 16 * 2 * GROUPS)

        @block.gpsimd
        def _(pool):
            nc.gpsimd.memset(ident[:], 0.0).then_inc(const_base, 1)
            nc.gpsimd.memset(until[:], 1.0).then_inc(const_base, 1)
            nc.gpsimd.memset(beyond[:], 1.0).then_inc(const_base, 1)
            nc.gpsimd.memset(ebd[:], 0.0).then_inc(const_ready, 1)
            nc.gpsimd.memset(powers[:, 0:1], 0.5).then_inc(const_ready, 1)
            nc.gpsimd.memset(powers[:, 1:2], -0.5).then_inc(const_ready, 1)
            nc.gpsimd.memset(unit[:, HI, :], 1.0).then_inc(const_ready, 1)
            nc.gpsimd.memset(unit[:, LO, :], 0.0).then_inc(const_ready, 1)
            pool.wait_ge(const_base, 3)
            pool.wait_ge(const_ready, 5)
            nc.gpsimd.affine_select(out=ident[:], in_=ident[:], compare_op=ALU.not_equal, fill=1.0, base=0,
                                    pattern=[[1, P]], channel_multiplier=-1).then_inc(const_ready, 1)
            for b in range(2):
                own = slice(b * S, (b + 1) * S)
                pool.wait_ge(const_ready, 6 + 2 * b)
                nc.gpsimd.affine_select(out=until[own, :], in_=until[own, :], compare_op=ALU.is_ge, fill=0.0, base=0,
                                        pattern=[[-1, S]], channel_multiplier=1).then_inc(const_ready, 1)
                pool.wait_ge(const_ready, 7 + 2 * b)
                nc.gpsimd.affine_select(out=beyond[own, :], in_=beyond[own, :], compare_op=ALU.is_gt, fill=0.0, base=0,
                                        pattern=[[1, S]], channel_multiplier=-1).then_inc(const_ready, 1)
            pool.wait_ge(const_ready, 10)

            def walk(part, G):
                first, end, looped, steps, _, _ = part
                for step in steps:
                    kind = step[0]
                    if kind == "C":
                        t = step[1]
                        pool.wait_ge(c_var, tile_count(G, t + 1))
                        nc.gpsimd.tensor_tensor(col[:, STD, t:t + 1], col[:, VAR, t:t + 1], powers[:, 0:1],
                                                ALU.pow).then_inc(c_std, 1)
                    if kind == "X":
                        t = step[1]
                        pool.wait_ge(x_var, tile_count(G + step[2], t + 1))
                        nc.gpsimd.tensor_tensor(col[:, XRSTD, t:t + 1], col[:, XVAR, t:t + 1], powers[:, 1:2],
                                                ALU.pow).then_inc(x_rstd, 1)

            each_part(pool, walk)

        @block.tensor
        def _(pe):
            pe.wait_ge(const_ready, 10)

            def transposes(part, G, step, source):
                for half in range(2):
                    pe.wait_ge(c_clear, ring_after(part, G, step, half - 1) + C_BANKS)
                    for j in range(HC):
                        kc = half * HC + j
                        last = nc.tensor.transpose(pc[:, half, j * P:(j + 1) * P], source[:, kc * P:(kc + 1) * P],
                                                   ident[:])
                    last.then_inc(c_full, 1)

            def project(k, t0, t1, c0, c1):
                oc, lr = k // 2, k % 2
                for kc in range(c0, c1):
                    for n, (a, b) in enumerate(PASSES):
                        last = nc.tensor.matmul(pm[:, k % M_BANKS, t0 * P:t1 * P], wt[:, lr, a, kc, oc * P:(oc + 1) * P],
                                                ht[:, kc, t0:t1, b, :], start=(kc == 0 and n == 0),
                                                stop=(kc == KC - 1 and n == len(PASSES) - 1))
                return last

            def walk(part, G):
                first, end, looped, steps, _, _ = part
                N = G + 1
                next_layer = 1 if first + 1 >= PER else 0
                fresh = first in (-1, PER - 1)
                for step in steps:
                    kind = step[0]
                    if kind == "T":
                        t = step[1]
                        if first + 1 < PER:
                            pe.wait_ge(x_norm, tile_count(N, t + 1))
                        else:
                            pe.wait_ge(x_loaded[H_SLOTS[t]], x_load_count(N, t))
                        transposes(part, G, step, rows[:, H_SLOTS[t], :])
                    elif kind == "W":
                        _, slot, count = w_slot(first, step)
                        pe.wait_ge(w_loaded[slot], count)
                        transposes(part, G, step, side[:, slot, :])
                    elif kind == "M":
                        k, t0, t1, c0, c1 = step[1:]
                        if t0 == 0 and c0 == 0:
                            pe.wait_ge(m_clear, M_JOBS * N + k - M_BANKS + 1 + M_BANKS)
                            if fresh:
                                pe.wait_ge(v_split, kind_count(first, ("V", k % 2, k // 2)))
                        if k < 2:
                            pe.wait_ge(c_clear, ring_after(part, G, ("T", t1 - 1)) + C_BANKS)
                        last = project(*step[1:])
                        if t1 == TILES and c1 == KC:
                            last.then_inc(m_full, 1)
                    elif kind == "S":
                        oc = step[1]
                        Q = G if oc == KC - 1 else N
                        pe.wait_ge(m_clear, M_JOBS * Q + 2 * oc + 2 + M_BANKS)
                        if oc == 0:
                            pe.wait_ge(mask_ready, mask_count(next_layer, N))
                        for t in range(TILES):
                            for b in range(2):
                                own = slice(t * P + b * S, t * P + (b + 1) * S)
                                h_parts = ht[:, oc, t].rearrange("p a (n b) -> p b (a n)", b=2)
                                last = nc.tensor.matmul(
                                    pu[:, t, b * 2 * P:(b + 1) * 2 * P], h_parts[:, b, :], gt[:, oc % 2, :, :, own],
                                    start=(oc == 0 and b == 0), stop=(oc == KC - 1), skip_group_check=True)
                            if oc == KC - 1:
                                last.then_inc(u_full, 1)
                    elif kind == "H":
                        t, half = step[1:]
                        j = H_JOB + 2 * t + half
                        pe.wait_ge(m_clear, M_JOBS * G + j - M_BANKS + 1 + M_BANKS)
                        n = 0
                        for kc in range(KC):
                            for a, b in PASSES:
                                last = nc.tensor.matmul(
                                    pm[:, j % M_BANKS, 0:HALF], ht[:, kc, t, a, :],
                                    wt[:, LIN, b, kc, half * HALF:(half + 1) * HALF],
                                    start=(n == 0), stop=(n == 3 * KC - 1))
                                n += 1
                        last.then_inc(m_full, 1)
                    elif kind == "A" and next_layer == 0:
                        pe.wait_ge(adj_loaded, 32 * N + 32)
                        wait_from(pe, u_joined, pair_count(N, 0, 2))
                        for t in range(TILES):
                            both = mask[:, t, ADJ:MR + 1, :].rearrange("p a b -> p (a b)")
                            last = nc.tensor.transpose(pu[:, t, 0:P], both, ident[:])
                        last.then_inc(a_full, 1)
                    elif kind == "C":
                        t = step[1]
                        if first == 0 and t == 0:
                            pe.wait_ge(unit_ready, 6)
                        pe.wait_ge(et_split, G + 1)
                        pe.wait_ge(m_clear, M_JOBS * G + H_JOB + 2 * t + 2 + M_BANKS)
                        for half in range(2):
                            pe.wait_ge(c_clear, ring_after(part, G, step, half - 1) + C_BANKS)
                            own = slice(0, SUMS + HALF) if half == 0 else slice(SUMS + HALF, SUMS + H)
                            for n, (a, b) in enumerate(PASSES):
                                last = nc.tensor.matmul(pc[:, half, 0:own.stop - own.start], et[:, t, a, :],
                                                        hl[:, H_SLOTS[t], b, own], start=(n == 0), stop=(n == 2))
                            last.then_inc(c_full, 1)
                if fresh:
                    pe.wait_ge(c_clear, ring_after(part, G, [s for s in steps if s[0] == "W"][-1]) + C_BANKS)

            each_part(pe, walk)

        @block.scalar
        def _(act):
            act.wait_ge(const_ready, 10)
            for slot in range(3):
                for part in (HI, LO):
                    nc.scalar.copy(hl[:, slot, part, 0:SUMS], unit[:, part, :]).then_inc(unit_ready, 1)

            def walk(part, G):
                first, end, looped, steps, _, _ = part
                N = G + 1
                layer = 1 if first >= PER else 0
                for step in steps:
                    kind = step[0]
                    if kind in ("T", "W"):
                        for half in range(2):
                            act.wait_ge(c_full, ring_after(part, G, step, half + 1))
                            src = pc[:, half, 0:HALF].rearrange("p (c n) -> p c n", c=HC)
                            if kind == "T":
                                nc.scalar.copy(ht_half(step[1], half, HI), by_graph(src)).then_inc(ht_hi, 1)
                            else:
                                mat, ob = step[1:]
                                dst = wt[:, mat, HI, half * HC:(half + 1) * HC, ob * P:(ob + 1) * P]
                                nc.scalar.copy(dst, src).then_inc(w_hi, 1)
                        if kind == "W" and next_block(first, step):
                            load_weights(act, next_block(first, step))
                    elif kind == "V":
                        _, slot, count = w_slot(first, step)
                        act.wait_ge(w_loaded[slot], count)
                        _, mat, ob = step
                        nc.scalar.copy(wt[:, mat, HI, :, ob * P:(ob + 1) * P],
                                       side[:, slot, :].rearrange("p (c n) -> p c n", c=KC)).then_inc(v_hi, 1)
                    elif kind == "M" and step[3] == TILES and step[5] == KC:
                        k = step[1]
                        act.wait_ge(m_full, M_JOBS * N + k + 1)
                        nc.scalar.copy(gt_part(k, HI), by_node(pm[:, k % M_BANKS, :])).then_inc(m_hi, 1)
                    elif kind == "H":
                        t, half = step[1:]
                        j = H_JOB + 2 * t + half
                        act.wait_ge(m_full, M_JOBS * G + j + 1)
                        nc.scalar.copy(hl[:, H_SLOTS[t], HI, SUMS + half * HALF:SUMS + (half + 1) * HALF],
                                       pm[:, j % M_BANKS, 0:HALF]).then_inc(m_hi, 1)
                    elif kind == "U":
                        p = step[1]
                        wait_from(act, stored[p], 32 * G)
                        act.wait_ge(u_full, tile_count(G, 2 * p + 2))
                        for b in range(2):
                            near, far = slice(b * S, (b + 1) * S), slice((1 - b) * S, (2 - b) * S)
                            nc.scalar.copy(parted[p][near].rearrange("p t a m j -> p t (a m j)"),
                                           pu[far, 2 * p:2 * p + 2, b * 2 * P:(b + 1) * 2 * P]).then_inc(u_cross, 1)
                    elif kind == "EX":
                        act.wait_ge(u_summed, pair_count(G, 2))
                        nc.scalar.activation(us[:], us[:], ACT.Exp, scale=INV_TEMPER).then_inc(e_exp, 1)
                    elif kind == "ET":
                        act.wait_ge(e_moved, 32 * G + 32)
                        nc.scalar.copy(et[:, :, HI, :], ebd[:]).then_inc(et_hi, 1)
                    elif kind == "N":
                        t = step[1]
                        act.wait_ge(x_shift, tile_count(G + step[2], t + 1))
                        row = rows[:, H_SLOTS[t], :]
                        nc.scalar.activation(row, row, ACT.Relu, bias=col[:, XSHIFT, t:t + 1],
                                             scale=col[:, XRSTD, t:t + 1]).then_inc(x_norm, 1)
                    elif kind == "F" and layer == 0:
                        t = step[1]
                        act.wait_ge(f_affine, tile_count(G, t + 1))
                        nc.scalar.activation(side[:, t % 2, :], side[:, t % 2, :], ACT.Relu).then_inc(f_done, 1)

            each_part(act, walk)

        @block.vector
        def _(dve):
            nc.vector.memset(us[:, 0, 0:1], 0.0).then_inc(m_clear, M_BANKS)
            nc.vector.memset(us[:, 0, 1:2], 0.0).then_inc(c_clear, C_BANKS)
            dve.wait_ge(const_ready, 10)

            def low_part(dst, src, hi):
                return nc.vector.tensor_tensor(dst, src, hi.bitcast(F32), ALU.subtract)

            def walk(part, G):
                first, end, looped, steps, _, _ = part
                N = G + 1
                layer = 1 if first >= PER else 0
                for step in steps:
                    kind = step[0]
                    if kind in ("T", "W"):
                        for half in range(2):
                            src = pc[:, half, 0:HALF].rearrange("p (c n) -> p c n", c=HC)
                            if kind == "T":
                                t = step[1]
                                dve.wait_ge(ht_hi, tile_count(N, t, 2) + half + 1)
                                op = low_part(ht_half(t, half, LO), by_graph(src), ht_half(t, half, HI))
                            else:
                                mat, ob = step[1:]
                                dve.wait_ge(w_hi, 2 * kind_count(first, step) + half - 1)
                                at = (slice(half * HC, (half + 1) * HC), slice(ob * P, (ob + 1) * P))
                                op = low_part(wt[:, mat, LO, at[0], at[1]], src, wt[:, mat, HI, at[0], at[1]])
                            op.then_inc(c_clear, 1)
                    elif kind == "V":
                        _, mat, ob = step
                        at = slice(ob * P, (ob + 1) * P)
                        dve.wait_ge(v_hi, kind_count(first, step))
                        low_part(wt[:, mat, LO, :, at],
                                 side[:, w_slot(first, step)[1], :].rearrange("p (c n) -> p c n", c=KC),
                                 wt[:, mat, HI, :, at]).then_inc(v_split, 1)
                    elif kind == "M" and step[3] == TILES and step[5] == KC:
                        k = step[1]
                        dve.wait_ge(m_hi, M_JOBS * N + k + 1)
                        low_part(gt_part(k, LO), by_node(pm[:, k % M_BANKS, :]), gt_part(k, HI)).then_inc(m_clear, 1)
                    elif kind == "H":
                        t, half = step[1:]
                        j = H_JOB + 2 * t + half
                        dve.wait_ge(m_hi, M_JOBS * G + j + 1)
                        at = slice(SUMS + half * HALF, SUMS + (half + 1) * HALF)
                        low_part(hl[:, H_SLOTS[t], LO, at], pm[:, j % M_BANKS, 0:HALF],
                                 hl[:, H_SLOTS[t], HI, at]).then_inc(m_clear, 1)
                    elif kind == "A" and first + 1 >= PER:
                        dve.wait_ge(adj_loaded, 32 * N + 32)
                        for made, source, keep in ((ML, ADJ, until), (MR, MR, beyond)):
                            nc.vector.tensor_tensor(mask[:, :, made, :], mask[:, :, source, :],
                                                    keep[:].unsqueeze(1).to_broadcast([P, TILES, S]),
                                                    ALU.mult).then_inc(mask_ready, 1)
                    elif kind == "A":
                        dve.wait_ge(a_full, N + 1)
                        nc.vector.tensor_tensor(mask[:, :, MR, :], mask[:, :, MR, :],
                                                beyond[:].unsqueeze(1).to_broadcast([P, TILES, S]),
                                                ALU.mult).then_inc(mask_ready, 1)
                        for b in range(2):
                            own = slice(b * S, (b + 1) * S)
                            nc.vector.tensor_copy(mask[own, :, ADJ, :], pu[own, :, own]).then_inc(mask_ready, 1)
                            nc.vector.tensor_tensor(mask[own, :, ML, :], pu[own, :, own],
                                                    until[own, :].unsqueeze(1).to_broadcast([S, TILES, S]),
                                                    ALU.mult).then_inc(mask_ready, 1)
                    elif kind == "U":
                        p = step[1]
                        pair = slice(2 * p, 2 * p + 2)
                        if p == 0:
                            dve.wait_ge(mask_ready, mask_count(layer, G))
                        dve.wait_ge(u_cross, pair_count(G, p + 1, 2))
                        for b in range(2):
                            near = slice(b * S, (b + 1) * S)
                            both = parted[p][near].rearrange("p t a m j -> p t (a m j)")
                            nc.vector.tensor_tensor(both, pu[near, pair, b * 2 * P:(b + 1) * 2 * P], both,
                                                    ALU.add).then_inc(u_joined, 1)
                        whole = parted[p][:, :, HI]
                        dve.wait_ge(u_joined, pair_count(G, p + 1, 2))
                        nc.vector.tensor_tensor(whole, whole, parted[p][:, :, LO], ALU.add).then_inc(u_whole, 1)
                        dve.wait_ge(u_whole, pair_count(G, p + 1))
                        nc.vector.tensor_tensor(whole, whole, mask[:, pair, ML:MR + 1:2, :],
                                                ALU.mult).then_inc(u_masked, 1)
                        dve.wait_ge(u_masked, pair_count(G, p + 1))
                        nc.vector.tensor_tensor(us[:, pair, :], whole[:, :, LEFT, :], whole[:, :, RIGHT, :],
                                                ALU.add).then_inc(u_summed, 1)
                    elif kind == "EM":
                        dve.wait_ge(e_exp, G + 1)
                        nc.vector.tensor_tensor(us[:], us[:], mask[:, :, ADJ, :], ALU.mult).then_inc(e_masked, 1)
                    elif kind == "ET":
                        dve.wait_ge(et_hi, G + 1)
                        low_part(et[:, :, LO, :], ebd[:], et[:, :, HI, :]).then_inc(et_split, 1)
                    elif kind == "C":
                        t = step[1]
                        if t == 0:
                            dve.wait_ge(vec_loaded, 48 * (layer + 1))
                        if t >= 2 and first < GROUPS - 1:
                            dve.wait_ge(stored[t % 2], 32 * G + 16)
                        context = result(part, t)
                        dve.wait_ge(c_full, ring_after(part, G, step, 1))
                        nc.vector.tensor_copy(col[:, ESUM, t:t + 1], pc[:, 0, 0:1]).then_inc(c_sum, 1)
                        dve.wait_ge(c_sum, tile_count(G, t + 1))
                        for half in range(2):
                            at = slice(half * HALF, (half + 1) * HALF)
                            behind = SUMS if half == 0 else 0
                            if half == 1:
                                dve.wait_ge(c_full, ring_after(part, G, step, 2))
                            nc.vector.scalar_tensor_tensor(
                                out=context[:, at], in0=vec[:, 0, at], scalar=col[:, ESUM, t:t + 1],
                                in1=pc[:, half, behind:behind + HALF], op0=ALU.mult, op1=ALU.add).then_inc(c_clear, 1)
                        wait_from(dve, c_moments, tile_count(G, t))
                        for half in range(2):
                            dve.wait_ge(c_clear, ring_after(part, G, step, half + 1) + C_BANKS)
                            nc.vector.bn_stats(stats[:, half, :], context[:, half * HALF:(half + 1) * HALF]
                                               ).then_inc(c_stats, 1)
                        dve.wait_ge(c_stats, tile_count(G, t + 1, 2))
                        nc.vector.tensor_scalar(col[:, FLOOR, t:t + 1], col[:, ESUM, t:t + 1], EPS_SUM, EPS_STD,
                                                ALU.add, ALU.mult).then_inc(c_floor, 1)
                        nc.vector.bn_aggr(mom[:, t, :], stats[:].rearrange("p a b -> p (a b)")).then_inc(c_moments, 1)
                        dve.wait_ge(c_moments, tile_count(G, t + 1))
                        nc.vector.tensor_scalar(col[:, VAR, t:t + 1], mom[:, t, 1:2], DDOF, None,
                                                ALU.mult).then_inc(c_var, 1)
                    elif kind == "F":
                        t = step[1]
                        n = tile_count(G, t + 1)
                        row = result(part, t)
                        nc.vector.scalar_tensor_tensor(out=row, in0=row, scalar=mom[:, t, 0:1], in1=vec[:, 1, :],
                                                       op0=ALU.subtract, op1=ALU.mult).then_inc(f_centred, 1)
                        dve.wait_ge(c_std, n)
                        dve.wait_ge(c_floor, n)
                        nc.vector.tensor_tensor(col[:, DEN, t:t + 1], col[:, STD, t:t + 1], col[:, FLOOR, t:t + 1],
                                                ALU.add).then_inc(c_den, 1)
                        dve.wait_ge(c_den, n)
                        nc.vector.reciprocal(col[:, SCALE, t:t + 1], col[:, DEN, t:t + 1]).then_inc(c_scale, 1)
                        dve.wait_ge(c_scale, n)
                        dve.wait_ge(f_centred, n)
                        nc.vector.scalar_tensor_tensor(out=row, in0=row, scalar=col[:, SCALE, t:t + 1],
                                                       in1=vec[:, 2, :], op0=ALU.mult, op1=ALU.add).then_inc(f_affine, 1)
                        if layer:
                            dve.wait_ge(f_affine, n)
                            dve.wait_ge(res_loaded[t % 2], 32 * (G - PER) + 16 * (t // 2) + 16)
                            nc.vector.scalar_tensor_tensor(out=row, in0=row, scalar=0.0, in1=side[:, 2 + t % 2, :],
                                                           op0=ALU.max, op1=ALU.add).then_inc(f_done, 1)
                    elif kind == "X":
                        t = step[1]
                        X = G + step[2]
                        dve.wait_ge(x_loaded[H_SLOTS[t]], x_load_count(X, t))
                        wait_from(dve, x_moments, tile_count(X, t))
                        for half in range(2):
                            nc.vector.bn_stats(xstats[:, half, :],
                                               rows[:, H_SLOTS[t], half * HALF:(half + 1) * HALF]).then_inc(x_stats, 1)
                        dve.wait_ge(x_stats, tile_count(X, t + 1, 2))
                        nc.vector.memset(col[:, XVAR, t:t + 1], EPS_LN).then_inc(x_eps, 1)
                        nc.vector.bn_aggr(xmom[:, t, :], xstats[:].rearrange("p a b -> p (a b)")).then_inc(x_moments, 1)
                        dve.wait_ge(x_moments, tile_count(X, t + 1))
                        dve.wait_ge(x_eps, tile_count(X, t + 1))
                        nc.vector.tensor_tensor(col[:, XVAR, t:t + 1], xmom[:, t, 1:2], col[:, XVAR, t:t + 1],
                                                ALU.add).then_inc(x_var, 1)
                    elif kind == "N":
                        t = step[1]
                        X = G + step[2]
                        dve.wait_ge(x_rstd, tile_count(X, t + 1))
                        nc.vector.scalar_tensor_tensor(out=col[:, XSHIFT, t:t + 1], in0=xmom[:, t, 0:1], scalar=-1.0,
                                                       in1=col[:, XRSTD, t:t + 1], op0=ALU.mult,
                                                       op1=ALU.mult).then_inc(x_shift, 1)

            each_part(dve, walk)


_INS = ["x", "adj", "L0_gnn_W_left", "L0_gnn_W_right", "L0_gnn_W_lin", "L0_gnn_b_lin", "L0_gnn_ln_a", "L0_gnn_ln_b"]


def kernel(**inputs):
    import numpy as _np
    import concourse.bacc as _bacc
    from concourse import mybir as _mybir
    from concourse.bass_utils import run_bass_kernel_spmd as _run

    nc = _bacc.Bacc("TRN2", target_bir_lowering=False, num_devices=1)
    arrays, args = {}, []
    for name in _INS:
        a = _np.ascontiguousarray(inputs[name])
        arrays[f"in_{name}_dram"] = a
        args.append(nc.dram_tensor(f"in_{name}_dram", a.shape, _mybir.dt.from_np(a.dtype), kind="ExternalInput").ap())
    shape = inputs["x"].shape
    h1 = nc.dram_tensor("h1_dram", (shape[0] * shape[1], shape[2]), _mybir.dt.float32, kind="Internal").ap()
    out = nc.dram_tensor("out_0_dram", shape, _mybir.dt.float32, kind="ExternalOutput").ap()
    graphs = 2 * TILES
    adj_t = nc.dram_tensor("adj_t_dram", (shape[0] // graphs, 2 * shape[1], TILES, shape[1]), _mybir.dt.float32,
                           kind="Internal").ap()
    gnn_kernel(nc, *args, h1, adj_t, out)
    r = _run(nc, [arrays], core_ids=[0])
    return r.results[0]["out_0_dram"]
```
